# Optimizing a Trainium2 kernel written in Bass

```python
import numpy as np
import jax
import jax.numpy as jnp

def _softmax(x, axis=-1):
    return jax.nn.softmax(x, axis=axis)

def _gelu(x):
    return jax.nn.gelu(x, approximate=True)

def _silu(x):
    return jax.nn.silu(x)

def _sigmoid(x):
    return jax.nn.sigmoid(x)

def _layernorm(x, axis=-1, eps=1e-05):
    m = jnp.mean(x, axis=axis, keepdims=True)
    v = jnp.var(x, axis=axis, keepdims=True)
    return (x - m) / jnp.sqrt(v + eps)

def _scatter_add(tgt, idx, src, axis=0):
    return tgt.at[idx].add(src)

def _segment_sum(src, seg, n):
    return jax.ops.segment_sum(src, seg, n)
kernel_name = 'mk_xattn_seq_d2_seqx_r8_c0707b'

def setup_inputs(seed: int=0):
    np.random.seed(seed)
    _w = jnp.asarray

    def _rec_inputs():
        import jax
        import jax.numpy as jnp
        _rk = jax.random.key(seed)
        x = 7.22e-05 + 1 * jax.random.normal(jax.random.fold_in(_rk, 1), (4, 256, 128), jnp.float32)
        _lenS = 256 - jax.random.randint(jax.random.fold_in(_rk, 7), (4,), 0, max(1, 256 // 4) + 1, jnp.int32)
        _lenS2 = 256 - jax.random.randint(jax.random.fold_in(_rk, 8), (4,), 0, max(1, 256 // 4) + 1, jnp.int32)
        _ctx_768P = jax.random.normal(jax.random.fold_in(_rk, 11), (4, 16, 96), jnp.float32)
        _ctx_768c = jax.random.dirichlet(jax.random.fold_in(_rk, 511), 0.3 * jnp.ones((16,), jnp.float32), (4, 256))
        _ctx_768t = jnp.einsum('bsk,bkd->bsd', _ctx_768c, _ctx_768P)
        _ctx_768t = _ctx_768t * jax.lax.rsqrt(jnp.mean(jnp.square(_ctx_768t)) + 1e-12) * 0.953939
        ctx_768 = -0.00055796 + 0.999787 * (_ctx_768t + 0.3 * jax.random.normal(jax.random.fold_in(_rk, 611), (4, 256, 96), jnp.float32))
        return (x, ctx_768)
    x, ctx_768 = _rec_inputs()

    def _L0_xattn_setup():
        import jax, jax.numpy as jnp
        import numpy as np
        D_MODEL = 128
        D_COND = 96
        N_HEADS = 16
        D_HEAD = 64
        D_ATTN = N_HEADS * D_HEAD
        D_FF = 4 * D_MODEL

        def _layernorm(x, g, b, eps=1e-05):
            mu = jnp.mean(x, axis=-1, keepdims=True)
            var = jnp.var(x, axis=-1, keepdims=True)
            return (x - mu) * jax.lax.rsqrt(var + eps) * g + b

        def _attention(xq, xkv, wq, wk, wv, wo, bo):
            B, S, _ = xq.shape
            T = xkv.shape[1]
            q = (xq @ wq).reshape(B, S, N_HEADS, D_HEAD)
            k = (xkv @ wk).reshape(B, T, N_HEADS, D_HEAD)
            v = (xkv @ wv).reshape(B, T, N_HEADS, D_HEAD)
            scale = D_HEAD ** (-0.5)
            attn = jnp.einsum('bihd,bjhd->bhij', q, k) * scale
            attn = jax.nn.softmax(attn, axis=-1)
            out = jnp.einsum('bhij,bjhd->bihd', attn, v).reshape(B, S, D_ATTN)
            return out @ wo + bo
        key = jax.random.key(seed)
        ks = jax.random.split(key, 16)
        B, S, T = (8, 128, 32)
        n = jax.random.normal
        inp = {'x': n(ks[0], (B, S, D_MODEL), jnp.float32), 'cond_emb': n(ks[1], (B, T, D_COND), jnp.float32), 'ln1_g': jnp.ones((D_MODEL,), jnp.float32), 'ln1_b': jnp.zeros((D_MODEL,), jnp.float32), 'ln2_g': jnp.ones((D_MODEL,), jnp.float32), 'ln2_b': jnp.zeros((D_MODEL,), jnp.float32), 'ln3_g': jnp.ones((D_MODEL,), jnp.float32), 'ln3_b': jnp.zeros((D_MODEL,), jnp.float32), 'sa_wq': n(ks[2], (D_MODEL, D_ATTN), jnp.float32) * D_MODEL ** (-0.5), 'sa_wk': n(ks[3], (D_MODEL, D_ATTN), jnp.float32) * D_MODEL ** (-0.5), 'sa_wv': n(ks[4], (D_MODEL, D_ATTN), jnp.float32) * D_MODEL ** (-0.5), 'sa_wo': n(ks[5], (D_ATTN, D_MODEL), jnp.float32) * D_ATTN ** (-0.5), 'sa_bo': jnp.zeros((D_MODEL,), jnp.float32), 'ca_wq': n(ks[6], (D_MODEL, D_ATTN), jnp.float32) * D_MODEL ** (-0.5), 'ca_wk': n(ks[7], (D_COND, D_ATTN), jnp.float32) * D_COND ** (-0.5), 'ca_wv': n(ks[8], (D_COND, D_ATTN), jnp.float32) * D_COND ** (-0.5), 'ca_wo': n(ks[9], (D_ATTN, D_MODEL), jnp.float32) * D_ATTN ** (-0.5), 'ca_bo': jnp.zeros((D_MODEL,), jnp.float32), 'ff_w1': n(ks[10], (D_MODEL, 2 * D_FF), jnp.float32) * D_MODEL ** (-0.5), 'ff_b1': jnp.zeros((2 * D_FF,), jnp.float32), 'ff_w2': n(ks[11], (D_FF, D_MODEL), jnp.float32) * D_FF ** (-0.5), 'ff_b2': jnp.zeros((D_MODEL,), jnp.float32)}
        return inp
    _L0_xattn_all = _L0_xattn_setup()
    _L0_xattn_in = {k: v for k, v in _L0_xattn_all.items() if k in ('ln1_g', 'ln1_b', 'ln2_g', 'ln2_b', 'ln3_g', 'ln3_b', 'sa_wq', 'sa_wk', 'sa_wv', 'sa_wo', 'sa_bo', 'ca_wq', 'ca_wk', 'ca_wv', 'ca_wo', 'ca_bo', 'ff_w1', 'ff_b1', 'ff_w2', 'ff_b2')}
    del _L0_xattn_all

    def _L1_xattn_setup():
        import jax, jax.numpy as jnp
        import numpy as np
        B, S, L = (2, 256, 64)
        WIDTH, HEADS, CTX = (128, 16, 96)
        HD = WIDTH // HEADS
        EPS = 1e-05

        def _layernorm(x, g, b):
            m = jnp.mean(x, axis=-1, keepdims=True)
            v = jnp.mean(jnp.square(x - m), axis=-1, keepdims=True)
            return (x - m) * jax.lax.rsqrt(v + EPS) * g + b

        def _mha(q_in, kv_in, wq, bq, wk, bk, wv, bv, wo, bo):
            b = q_in.shape[0]
            q = (q_in @ wq.T + bq).reshape(b, -1, HEADS, HD).transpose(0, 2, 1, 3)
            k = (kv_in @ wk.T + bk).reshape(b, -1, HEADS, HD).transpose(0, 2, 1, 3)
            v = (kv_in @ wv.T + bv).reshape(b, -1, HEADS, HD).transpose(0, 2, 1, 3)
            scores = jnp.einsum('bhqd,bhkd->bhqk', q, k) * HD ** (-0.5)
            p = jax.nn.softmax(scores, axis=-1)
            o = jnp.einsum('bhqk,bhkd->bhqd', p, v)
            o = o.transpose(0, 2, 1, 3).reshape(b, -1, WIDTH)
            return o @ wo.T + bo
        key = jax.random.key(seed)
        ks = jax.random.split(key, 32)

        def xav(k, shape, gain=1.0):
            fan_out, fan_in = shape
            a = gain * np.sqrt(6.0 / (fan_in + fan_out))
            return jax.random.uniform(k, shape, jnp.float32, -a, a)
        g2 = 1.0 / np.sqrt(2.0)
        inp = {'x': jax.random.normal(ks[0], (B, S, WIDTH), jnp.float32), 'context': jax.random.normal(ks[1], (B, L, CTX), jnp.float32), 'ln1_g': jnp.ones((WIDTH,), jnp.float32), 'ln1_b': jnp.zeros((WIDTH,), jnp.float32), 'ln2_g': jnp.ones((WIDTH,), jnp.float32), 'ln2_b': jnp.zeros((WIDTH,), jnp.float32), 'ln3_g': jnp.ones((WIDTH,), jnp.float32), 'ln3_b': jnp.zeros((WIDTH,), jnp.float32), 'sa_wq': xav(ks[2], (WIDTH, WIDTH), g2), 'sa_bq': jnp.zeros((WIDTH,), jnp.float32), 'sa_wk': xav(ks[3], (WIDTH, WIDTH), g2), 'sa_bk': jnp.zeros((WIDTH,), jnp.float32), 'sa_wv': xav(ks[4], (WIDTH, WIDTH), g2), 'sa_bv': jnp.zeros((WIDTH,), jnp.float32), 'sa_wo': xav(ks[5], (WIDTH, WIDTH), 1.0), 'sa_bo': jnp.zeros((WIDTH,), jnp.float32), 'ca_wq': xav(ks[6], (WIDTH, WIDTH), g2), 'ca_bq': jnp.zeros((WIDTH,), jnp.float32), 'ca_wk': xav(ks[7], (WIDTH, CTX), g2), 'ca_bk': jnp.zeros((WIDTH,), jnp.float32), 'ca_wv': xav(ks[8], (WIDTH, CTX), g2), 'ca_bv': jnp.zeros((WIDTH,), jnp.float32), 'ca_wo': xav(ks[9], (WIDTH, WIDTH), 1.0), 'ca_bo': jnp.zeros((WIDTH,), jnp.float32), 'mlp_w1': 0.02 * jax.random.normal(ks[10], (4 * WIDTH, WIDTH), jnp.float32), 'mlp_b1': jnp.zeros((4 * WIDTH,), jnp.float32), 'mlp_w2': 0.02 * jax.random.normal(ks[11], (WIDTH, 4 * WIDTH), jnp.float32), 'mlp_b2': jnp.zeros((WIDTH,), jnp.float32)}
        return inp
    _L1_xattn_all = _L1_xattn_setup()
    _L1_xattn_in = {k: v for k, v in _L1_xattn_all.items() if k in ('ln1_g', 'ln1_b', 'ln2_g', 'ln2_b', 'ln3_g', 'ln3_b', 'sa_wq', 'sa_bq', 'sa_wk', 'sa_bk', 'sa_wv', 'sa_bv', 'sa_wo', 'sa_bo', 'ca_wq', 'ca_bq', 'ca_wk', 'ca_bk', 'ca_wv', 'ca_bv', 'ca_wo', 'ca_bo', 'mlp_w1', 'mlp_b1', 'mlp_w2', 'mlp_b2')}
    del _L1_xattn_all
    return {'x': x, 'ctx_768': ctx_768, 'L0_xattn_ln1_g': _L0_xattn_in['ln1_g'], 'L0_xattn_ln1_b': _L0_xattn_in['ln1_b'], 'L0_xattn_ln2_g': _L0_xattn_in['ln2_g'], 'L0_xattn_ln2_b': _L0_xattn_in['ln2_b'], 'L0_xattn_ln3_g': _L0_xattn_in['ln3_g'], 'L0_xattn_ln3_b': _L0_xattn_in['ln3_b'], 'L0_xattn_sa_wq': _L0_xattn_in['sa_wq'], 'L0_xattn_sa_wk': _L0_xattn_in['sa_wk'], 'L0_xattn_sa_wv': _L0_xattn_in['sa_wv'], 'L0_xattn_sa_wo': _L0_xattn_in['sa_wo'], 'L0_xattn_sa_bo': _L0_xattn_in['sa_bo'], 'L0_xattn_ca_wq': _L0_xattn_in['ca_wq'], 'L0_xattn_ca_wk': _L0_xattn_in['ca_wk'], 'L0_xattn_ca_wv': _L0_xattn_in['ca_wv'], 'L0_xattn_ca_wo': _L0_xattn_in['ca_wo'], 'L0_xattn_ca_bo': _L0_xattn_in['ca_bo'], 'L0_xattn_ff_w1': _L0_xattn_in['ff_w1'], 'L0_xattn_ff_b1': _L0_xattn_in['ff_b1'], 'L0_xattn_ff_w2': _L0_xattn_in['ff_w2'], 'L0_xattn_ff_b2': _L0_xattn_in['ff_b2'], 'L1_xattn_ln1_g': _L1_xattn_in['ln1_g'], 'L1_xattn_ln1_b': _L1_xattn_in['ln1_b'], 'L1_xattn_ln2_g': _L1_xattn_in['ln2_g'], 'L1_xattn_ln2_b': _L1_xattn_in['ln2_b'], 'L1_xattn_ln3_g': _L1_xattn_in['ln3_g'], 'L1_xattn_ln3_b': _L1_xattn_in['ln3_b'], 'L1_xattn_sa_wq': _L1_xattn_in['sa_wq'], 'L1_xattn_sa_bq': _L1_xattn_in['sa_bq'], 'L1_xattn_sa_wk': _L1_xattn_in['sa_wk'], 'L1_xattn_sa_bk': _L1_xattn_in['sa_bk'], 'L1_xattn_sa_wv': _L1_xattn_in['sa_wv'], 'L1_xattn_sa_bv': _L1_xattn_in['sa_bv'], 'L1_xattn_sa_wo': _L1_xattn_in['sa_wo'], 'L1_xattn_sa_bo': _L1_xattn_in['sa_bo'], 'L1_xattn_ca_wq': _L1_xattn_in['ca_wq'], 'L1_xattn_ca_bq': _L1_xattn_in['ca_bq'], 'L1_xattn_ca_wk': _L1_xattn_in['ca_wk'], 'L1_xattn_ca_bk': _L1_xattn_in['ca_bk'], 'L1_xattn_ca_wv': _L1_xattn_in['ca_wv'], 'L1_xattn_ca_bv': _L1_xattn_in['ca_bv'], 'L1_xattn_ca_wo': _L1_xattn_in['ca_wo'], 'L1_xattn_ca_bo': _L1_xattn_in['ca_bo'], 'L1_xattn_mlp_w1': _L1_xattn_in['mlp_w1'], 'L1_xattn_mlp_b1': _L1_xattn_in['mlp_b1'], 'L1_xattn_mlp_w2': _L1_xattn_in['mlp_w2'], 'L1_xattn_mlp_b2': _L1_xattn_in['mlp_b2']}

def reference(x, ctx_768, L0_xattn_ln1_g, L0_xattn_ln1_b, L0_xattn_ln2_g, L0_xattn_ln2_b, L0_xattn_ln3_g, L0_xattn_ln3_b, L0_xattn_sa_wq, L0_xattn_sa_wk, L0_xattn_sa_wv, L0_xattn_sa_wo, L0_xattn_sa_bo, L0_xattn_ca_wq, L0_xattn_ca_wk, L0_xattn_ca_wv, L0_xattn_ca_wo, L0_xattn_ca_bo, L0_xattn_ff_w1, L0_xattn_ff_b1, L0_xattn_ff_w2, L0_xattn_ff_b2, L1_xattn_ln1_g, L1_xattn_ln1_b, L1_xattn_ln2_g, L1_xattn_ln2_b, L1_xattn_ln3_g, L1_xattn_ln3_b, L1_xattn_sa_wq, L1_xattn_sa_bq, L1_xattn_sa_wk, L1_xattn_sa_bk, L1_xattn_sa_wv, L1_xattn_sa_bv, L1_xattn_sa_wo, L1_xattn_sa_bo, L1_xattn_ca_wq, L1_xattn_ca_bq, L1_xattn_ca_wk, L1_xattn_ca_bk, L1_xattn_ca_wv, L1_xattn_ca_bv, L1_xattn_ca_wo, L1_xattn_ca_bo, L1_xattn_mlp_w1, L1_xattn_mlp_b1, L1_xattn_mlp_w2, L1_xattn_mlp_b2):
    import jax
    import jax.numpy as jnp

    def _L0_xattn_ref(x, cond_emb, ln1_g, ln1_b, ln2_g, ln2_b, ln3_g, ln3_b, sa_wq, sa_wk, sa_wv, sa_wo, sa_bo, ca_wq, ca_wk, ca_wv, ca_wo, ca_bo, ff_w1, ff_b1, ff_w2, ff_b2):
        import jax, jax.numpy as jnp
        import numpy as np
        D_MODEL = 128
        D_COND = 96
        N_HEADS = 16
        D_HEAD = 64
        D_ATTN = N_HEADS * D_HEAD
        D_FF = 4 * D_MODEL

        def _layernorm(x, g, b, eps=1e-05):
            mu = jnp.mean(x, axis=-1, keepdims=True)
            var = jnp.var(x, axis=-1, keepdims=True)
            return (x - mu) * jax.lax.rsqrt(var + eps) * g + b

        def _attention(xq, xkv, wq, wk, wv, wo, bo):
            B, S, _ = xq.shape
            T = xkv.shape[1]
            q = (xq @ wq).reshape(B, S, N_HEADS, D_HEAD)
            k = (xkv @ wk).reshape(B, T, N_HEADS, D_HEAD)
            v = (xkv @ wv).reshape(B, T, N_HEADS, D_HEAD)
            scale = D_HEAD ** (-0.5)
            attn = jnp.einsum('bihd,bjhd->bhij', q, k) * scale
            attn = jax.nn.softmax(attn, axis=-1)
            out = jnp.einsum('bhij,bjhd->bihd', attn, v).reshape(B, S, D_ATTN)
            return out @ wo + bo
        h = _layernorm(x, ln1_g, ln1_b)
        x = _attention(h, h, sa_wq, sa_wk, sa_wv, sa_wo, sa_bo) + x
        h = _layernorm(x, ln2_g, ln2_b)
        x = _attention(h, cond_emb, ca_wq, ca_wk, ca_wv, ca_wo, ca_bo) + x
        h = _layernorm(x, ln3_g, ln3_b)
        p = h @ ff_w1 + ff_b1
        a, gate = (p[..., :D_FF], p[..., D_FF:])
        h = a * jax.nn.gelu(gate, approximate=False) @ ff_w2 + ff_b2
        return h + x

    def _L1_xattn_ref(x, context, ln1_g, ln1_b, ln2_g, ln2_b, ln3_g, ln3_b, sa_wq, sa_bq, sa_wk, sa_bk, sa_wv, sa_bv, sa_wo, sa_bo, ca_wq, ca_bq, ca_wk, ca_bk, ca_wv, ca_bv, ca_wo, ca_bo, mlp_w1, mlp_b1, mlp_w2, mlp_b2):
        import jax, jax.numpy as jnp
        import numpy as np
        B, S, L = (2, 256, 64)
        WIDTH, HEADS, CTX = (128, 16, 96)
        HD = WIDTH // HEADS
        EPS = 1e-05

        def _layernorm(x, g, b):
            m = jnp.mean(x, axis=-1, keepdims=True)
            v = jnp.mean(jnp.square(x - m), axis=-1, keepdims=True)
            return (x - m) * jax.lax.rsqrt(v + EPS) * g + b

        def _mha(q_in, kv_in, wq, bq, wk, bk, wv, bv, wo, bo):
            b = q_in.shape[0]
            q = (q_in @ wq.T + bq).reshape(b, -1, HEADS, HD).transpose(0, 2, 1, 3)
            k = (kv_in @ wk.T + bk).reshape(b, -1, HEADS, HD).transpose(0, 2, 1, 3)
            v = (kv_in @ wv.T + bv).reshape(b, -1, HEADS, HD).transpose(0, 2, 1, 3)
            scores = jnp.einsum('bhqd,bhkd->bhqk', q, k) * HD ** (-0.5)
            p = jax.nn.softmax(scores, axis=-1)
            o = jnp.einsum('bhqk,bhkd->bhqd', p, v)
            o = o.transpose(0, 2, 1, 3).reshape(b, -1, WIDTH)
            return o @ wo.T + bo
        h = _layernorm(x, ln1_g, ln1_b)
        x = x + _mha(h, h, sa_wq, sa_bq, sa_wk, sa_bk, sa_wv, sa_bv, sa_wo, sa_bo)
        h = _layernorm(x, ln2_g, ln2_b)
        x = x + _mha(h, context, ca_wq, ca_bq, ca_wk, ca_bk, ca_wv, ca_bv, ca_wo, ca_bo)
        h = _layernorm(x, ln3_g, ln3_b)
        h = jax.nn.gelu(h @ mlp_w1.T + mlp_b1, approximate=False) @ mlp_w2.T + mlp_b2
        return x + h
    x = _L0_xattn_ref(x, ctx_768, L0_xattn_ln1_g, L0_xattn_ln1_b, L0_xattn_ln2_g, L0_xattn_ln2_b, L0_xattn_ln3_g, L0_xattn_ln3_b, L0_xattn_sa_wq, L0_xattn_sa_wk, L0_xattn_sa_wv, L0_xattn_sa_wo, L0_xattn_sa_bo, L0_xattn_ca_wq, L0_xattn_ca_wk, L0_xattn_ca_wv, L0_xattn_ca_wo, L0_xattn_ca_bo, L0_xattn_ff_w1, L0_xattn_ff_b1, L0_xattn_ff_w2, L0_xattn_ff_b2)
    x = _L1_xattn_ref(x, ctx_768, L1_xattn_ln1_g, L1_xattn_ln1_b, L1_xattn_ln2_g, L1_xattn_ln2_b, L1_xattn_ln3_g, L1_xattn_ln3_b, L1_xattn_sa_wq, L1_xattn_sa_bq, L1_xattn_sa_wk, L1_xattn_sa_bk, L1_xattn_sa_wv, L1_xattn_sa_bv, L1_xattn_sa_wo, L1_xattn_sa_bo, L1_xattn_ca_wq, L1_xattn_ca_bq, L1_xattn_ca_wk, L1_xattn_ca_bk, L1_xattn_ca_wv, L1_xattn_ca_bv, L1_xattn_ca_wo, L1_xattn_ca_bo, L1_xattn_mlp_w1, L1_xattn_mlp_b1, L1_xattn_mlp_w2, L1_xattn_mlp_b2)
    return x

_drawn_inputs = setup_inputs


def setup_inputs(seed=0):
    import zlib

    import numpy as np

    out = dict(_drawn_inputs(seed))
    spreads = {'L0_xattn_ln1_g': (1.0, 0.2),
     'L0_xattn_ln1_b': (0.0, 0.1),
     'L0_xattn_ln2_g': (1.0, 0.2),
     'L0_xattn_ln2_b': (0.0, 0.336),
     'L0_xattn_ln3_g': (1.0, 0.2),
     'L0_xattn_ln3_b': (0.0, 0.1),
     'L0_xattn_sa_bo': (0.0, 0.1),
     'L0_xattn_ca_bo': (0.0, 0.1),
     'L0_xattn_ff_b1': (0.0, 0.1),
     'L0_xattn_ff_b2': (0.0, 0.1),
     'L1_xattn_ln1_g': (1.0, 0.2),
     'L1_xattn_ln1_b': (0.0, 0.1),
     'L1_xattn_ln2_g': (1.0, 0.6),
     'L1_xattn_ln2_b': (0.0, 0.8),
     'L1_xattn_ln3_g': (1.0, 0.6),
     'L1_xattn_ln3_b': (0.0, 0.8),
     'L1_xattn_sa_bq': (0.0, 0.8),
     'L1_xattn_sa_bk': (0.0, 0.8),
     'L1_xattn_sa_bv': (0.0, 0.1),
     'L1_xattn_sa_bo': (0.0, 0.1),
     'L1_xattn_ca_bq': (0.0, 0.8),
     'L1_xattn_ca_bk': (0.0, 0.8),
     'L1_xattn_ca_bv': (0.0, 0.1),
     'L1_xattn_ca_bo': (0.0, 0.1),
     'L1_xattn_mlp_b1': (0.0, 0.451),
     'L1_xattn_mlp_b2': (0.0, 0.1)}
    factors = {}
    for name, (base, spread) in spreads.items():
        noise = np.random.default_rng([zlib.crc32(name.encode()), seed]).standard_normal(out[name].shape)
        drawn = base * np.exp(spread * noise) if base else spread * noise
        out[name] = jnp.asarray(drawn.astype(out[name].dtype))
    for name, factor in factors.items():
        out[name] = (out[name] * factor).astype(out[name].dtype)
    return out
```

```python
from contextlib import ExitStack

import numpy as np
import concourse.bass as bass
from concourse import mybir

F32 = mybir.dt.float32
F32R = mybir.dt.float32r
ACT = mybir.ActivationFunctionType
ALU = mybir.AluOpType
AX = mybir.AxisListType

P = 128
BATCHES, S, D, DC = 4, 256, 128, 96
STREAMS = 2
ITERATIONS = BATCHES // STREAMS
HEADS = 16
PAIRS = HEADS // 2
QUADS = HEADS // 4
HD = (64, 8)
SLOT = 32
DF = 512
TT = S // P
EPS = 1e-5
EXP_SCALE = (64 ** -0.5, 8 ** -0.5)

UNITS = [(layer, cross, s) for layer in (0, 1) for cross in (0, 1) for s in range(STREAMS)]

LN_G, LN_B = 0, 6
FF_B1 = 12
MLP_B1 = 20
QK_B = 24
QK_BM = 40
MASK = 56
N_COLS = 58


def attention(u):
    tasks = []
    for t in range(PAIRS):
        tasks += [("scores", u, TT * t + kb) for kb in range(TT)]
        if t == 0 and u >= 1:
            tasks.append(("pv", u - 1, QUADS - 1))
        if t >= 2 and t % 2 == 0:
            tasks.append(("pv", u, t // 2 - 1))
    return tasks


def tail(u):
    layer, cross, _ = UNITS[u]
    tasks = [("rd", u, 0)] + [("r", u, i) for i in range(4 if layer == 0 else 2)] + [("o", u, 0)]
    if cross:
        tasks += [("ln", u, layer * 3 + 2)] + [("up", u, i) for i in range(4 if layer == 0 else 2)] + [("down", u, 0)]
    return tasks


def head(u):
    layer, cross, _ = UNITS[u]
    smax = [("smax", u, t) for t in range(PAIRS)]
    if layer == 1:
        return [("ln", u, 3 + cross)] + [("qk", u, i) for i in (0, 2, 1, 3)] + smax + [("mt", u, 0)]
    tasks = [("ln", u, cross), ("g", u, 0)]
    for t in range(1, PAIRS):
        tasks += [("g", u, t), smax[t - 1]]
    return tasks + [smax[-1], ("mt", u, 0)]


def values(u):
    return [("v", u, i) for i in range(4 if UNITS[u][0] == 0 else TT)]


ORDER = [
    "sssvsssssssssssssssvsvsv",
    "mmmsmmmssmsmmssmsmsmsmmssmsmssmmmsvsvsvsv",
    "mmmmmsvmssssmsmsmmsmmssmsmssmssmssmmssmmsssvsvsv",
    "mmmmsvmmssssmsmmsmmsmssmssmmsmssmsmsmssmsssvsvsv",
    "mmmmmmsssssmsmmmmsmssmssmsmmsssmssmsvsmssssssmsv",
    "mmmsmmmssssmsmsmsssssmsssmmssmsmmssmsmssvsmsmmsv",
    "mmmsvmmmsssmmmsvssmmssmmsmssmsmsmsmsmsms",
    "mmmsmvmmmssvsmmsmssmmssmsmsmssmsmssmsmms",
    "mmmsmmmssmsmmmmsmmmmmmmmmsss",
    "sssssssss",
]


def strands(p):
    n = len(UNITS)
    main = attention(p) if 0 <= p < n else []
    side, val = [], []
    if p == -1:
        side += [("ctx", s, 0) for s in range(STREAMS)]
    if p == n:
        side += [("pv", p - 1, QUADS - 1)]
    if p >= 1:
        side += tail(p - 1)
    if p + 1 < n:
        side += head(p + 1)
        val = values(p + 1)
    return {"m": main, "s": side, "v": val}


def plan():
    tasks = []
    for p, order in zip(range(-1, len(UNITS) + 1), ORDER, strict=True):
        left = strands(p)
        for c in order:
            tasks.append(left[c].pop(0))
        assert not any(left.values())
    return tasks


def signals_of(task):
    kind, u, i = task
    layer, cross, _ = UNITS[u]
    if kind == "ctx":
        return [("side_ready", 0), ("h32_ready", 0), ("split_hi", 0), ("split_ready", 0)]
    if kind == "ln":
        own = [("stats_done", 0), ("mean_var", 0), ("var_eps", 0), ("rstd_ready", 0), ("z_ready", 0), ("x_bias", 0), ("side_ready", 0), ("h32_ready", 0)]
        return own + ([("split_hi", 0), ("split_ready", 0)] if i < 2 else [])
    return {
        "g": [("side_ready", 0), ("g_hi_ready", 0), ("g_lo_ready", 0)],
        "qk": [("side_ready", 0), ("qk_hi", 0), ("qk_ready", 0)],
        "v": [("side_ready", 0), ("v0_ready" if layer == 0 else "v1_ready", 0)],
        "smax": [("smax_ready", 0), ("smax_ready", 1), ("max_done", 0), ("max_done", 1)],
        "mt": [("max_hi", 0), ("max_parts", 0), ("side_ready", 0), ("mt_ready", 0)],
        "scores": [("scores_ready", 0), ("probs_ready", 0)] + [("presum", 0)] * (i % TT == TT - 1),
        "pv": [("quad_done", 0), ("o_copied", 0)],
        "rd": [("den_recip", 0), ("den_hi", 0), ("den_ready", 0)],
        "r": [("side_ready", 0), ("o_scaled", 0)],
        "o": [("side_ready", 0), ("x_ready", 0)],
        "up": [("side_ready", 0)] + ([("gelu", 0), ("act0_ready", 0)] if layer == 0 else [("act1_ready", 0)]),
        "down": [("side_ready", 0)] + ([("x_ready", 0)] if layer == 0 else [("out_ready", 0)]),
    }[kind]


RELEASE = {"ctx": "h32_ready", "ln": "h32_ready", "g": "g_lo_ready", "qk": "qk_ready", "mt": "mt_ready", "r": "o_scaled", "o": "x_ready"}


def release_of(task):
    kind, u, i = task
    layer = UNITS[u][0]
    if kind == "v":
        return "v0_ready" if layer == 0 else "v1_ready"
    if kind == "up":
        return "act0_ready" if layer == 0 else "act1_ready"
    if kind == "down":
        return "x_ready" if layer == 0 else "out_ready"
    return RELEASE[kind]


class Counts:

    def __init__(self, tasks):
        self.at, self.total, self.bank, self.before = {}, {}, {}, {}
        sides = []
        for task in tasks:
            for sig, part in signals_of(task):
                self.total[sig] = self.total.get(sig, 0) + 1
                self.at[sig, task, part] = self.total[sig]
                if sig == "side_ready":
                    self.bank[task] = len(sides) % 2
                    self.before[task] = sides[-2] if len(sides) >= 2 else None
                    sides.append(task)


def build(nc, x_in, ctx_in, wqT_sa, wkT_sa, wqT_ca, wkT_ca, wv0_sa, wv0_ca, wo0, w1_0, w2_0,
          wqk1_sa, wq1_ca, wk1_ca, wv1_sa, wv1_ca, wo1, w1_1, w2_1, cols_in, rows_in, vrows_in,
          ident_in, selneg_in, e_in, sel0_in, sel1_in, out):
    tasks = plan()
    counts = Counts(tasks)
    with ExitStack() as ctx:
        def sb(name, shape, dt=F32):
            return ctx.enter_context(nc.sbuf_tensor(name, shape, dt))

        A_hi = [sb("A_hi_sa", [P, HEADS, D], F32R), sb("A_hi_ca", [P, HEADS, DC], F32R)]
        A_lo = [sb("A_lo_sa", [P, HEADS, D], F32R), sb("A_lo_ca", [P, HEADS, DC], F32R)]
        wv0 = [sb("wv0_sa_s", [P, 1024]), sb("wv0_ca_s", [DC, 1024])]
        wo0_s = sb("wo0_s", [P, 2, 8, D])
        w1_0s = sb("w1_0s", [P, 2 * DF])
        w2_0s = sb("w2_0s", [P, 4, D])
        wqk1 = [sb("wqk1_sa_s", [P, 2, 512]), sb("wq1_ca_s", [P, 512])]
        wk1_cas = sb("wk1_ca_s", [DC, 512])
        wv1 = [sb("wv1_sa_s", [P, 512]), sb("wv1_ca_s", [DC, 512])]
        wo1_s = sb("wo1_s", [P, 2, 4, D])
        w1_1s = sb("w1_1s", [P, DF])
        w2_1s = sb("w2_1s", [P, 4, D])
        cols = sb("cols", [P, N_COLS])
        rows = sb("rows", [P, 6, D])
        vrows = sb("vrows", [P, 2, 512])
        ident = sb("ident", [P, P])
        selneg = sb("selneg", [P, PAIRS, P], F32R)
        e_cols = sb("e_cols", [P, QUADS, SLOT])
        sel0 = sb("sel0", [P, PAIRS, P], F32R)
        sel1 = sb("sel1", [P, QUADS, P], F32R)
        half_neg = sb("half_neg", [P, TT])

        X = [sb(f"x{s}", [P, TT, D]) for s in range(STREAMS)]
        XO = [sb(f"xo{s}", [P, TT, D]) for s in range(STREAMS)]
        C = [sb(f"c{s}", [P, TT, DC]) for s in range(STREAMS)]
        h_hi = [sb(f"h_hi{s}", [P, S], F32R) for s in range(STREAMS)]
        h_lo = [sb(f"h_lo{s}", [P, S], F32R) for s in range(STREAMS)]
        c32 = [sb(f"c32_{s}", [DC, S]) for s in range(STREAMS)]
        c_hi = [sb(f"c_hi{s}", [DC, S], F32R) for s in range(STREAMS)]
        c_lo = [sb(f"c_lo{s}", [DC, S], F32R) for s in range(STREAMS)]

        stats = sb("stats", [P, TT, 6])
        mv = sb("mv", [P, TT, 2])
        ve = sb("ve", [P, TT])
        rstd = sb("rstd", [P, TT])
        z = sb("z", [P, TT, D])
        h32 = sb("h32", [P, S])

        g_hi = sb("g_hi", [P, PAIRS, 2 * S], F32R)
        g_lo = sb("g_lo", [P, PAIRS, 2 * S], F32R)
        qk1 = [g_hi, g_lo]
        V = [sb(f"v{i}", [P, TT, 1024]) for i in range(2)]
        probs = sb("probs", [P, 4, TT, 2 * S])
        psums = sb("psums", [P, 2, 2 * S])
        o_un = sb("o_un", [P, PAIRS, S])
        rd = sb("rd", [P, S])
        rd_hi = sb("rd_hi", [P, S], F32R)
        rd_lo = sb("rd_lo", [P, S], F32R)
        mx = sb("mx", [P, TT, 2, PAIRS])
        mx_hi = sb("mx_hi", [P, TT, 2, PAIRS], F32R)
        mx_parts = sb("mx_parts", [P, TT, 2, 2, PAIRS])
        MT = [sb(f"mt{i}", [P, 2 * S], F32R) for i in range(2)]
        qk_low = sb("qk_low", [P, 2, 2, S])
        gate = sb("gate", [P, 2, S])
        hidden = sb("hidden", [P, 4, S])

        banks = [ctx.enter_context(nc.psum_tensor(f"bank{i}", [P, 512], F32)) for i in range(8)]
        max_bank = banks[0:2]
        score_bank = banks[2:4]
        pv_bank = banks[4]
        den_bank = banks[6]
        side_bank = [banks[5], banks[7]]

        sem = lambda name: ctx.enter_context(nc.semaphore(name))
        side_ready, smax_ready, scores_ready, quad_done = sem("side_ready"), sem("smax_ready"), sem("scores_ready"), sem("quad_done")
        stats_done, mean_var, var_eps, rstd_ready = sem("stats_done"), sem("mean_var"), sem("var_eps"), sem("rstd_ready")
        z_ready, h32_ready, split_hi, split_ready = sem("z_ready"), sem("h32_ready"), sem("split_hi"), sem("split_ready")
        g_hi_ready, g_lo_ready, qk_hi, qk_ready = sem("g_hi_ready"), sem("g_lo_ready"), sem("qk_hi"), sem("qk_ready")
        v0_ready, v1_ready = sem("v0_ready"), sem("v1_ready")
        max_done, max_hi, max_parts, mt_ready = sem("max_done"), sem("max_hi"), sem("max_parts"), sem("mt_ready")
        probs_ready, presum, o_copied = sem("probs_ready"), sem("presum"), sem("o_copied")
        den_recip, den_hi, den_ready, o_scaled = sem("den_recip"), sem("den_hi"), sem("den_ready"), sem("o_scaled")
        x_bias, x_ready, out_ready = sem("x_bias"), sem("x_ready"), sem("out_ready")
        gelu, act0_ready, act1_ready = sem("gelu"), sem("act0_ready"), sem("act1_ready")
        sems = {x.name: x for x in (
            side_ready, smax_ready, scores_ready, quad_done, stats_done, mean_var, var_eps, rstd_ready, z_ready, h32_ready,
            split_hi, split_ready, g_hi_ready, g_lo_ready, qk_hi, qk_ready, v0_ready, v1_ready, max_done, max_hi, max_parts,
            mt_ready, probs_ready, presum, o_copied, den_recip, den_hi, den_ready, o_scaled, x_bias, x_ready, out_ready,
            gelu, act0_ready, act1_ready)}
        assert set(counts.total) == set(sems)
        in_loaded = sem("in_loaded")
        stored = sem("stored")
        w_a = [sem("wqk_sa_loaded"), sem("wqk_ca_loaded")]
        w_rest, w_cast = sem("weights_loaded"), sem("selectors_loaded")
        consts_set = sem("consts_set")
        prep_ready, prep_hi, prep_lo = sem("prep_ready"), sem("prep_hi"), sem("prep_lo")
        loop_sems = [x.num for x in (*sems.values(), in_loaded, stored)]

        loads = [
            (wv0[0], wv0_sa), (wv0[1], wv0_ca), (wo0_s, wo0), (w1_0s, w1_0), (w2_0s, w2_0),
            (wqk1[0], wqk1_sa), (wqk1[1], wq1_ca), (wk1_cas, wk1_ca), (wv1[0], wv1_sa), (wv1[1], wv1_ca),
            (wo1_s, wo1), (w1_1s, w1_1), (w2_1s, w2_1),
        ]
        small = [(cols, cols_in), (ident, ident_in), (e_cols, e_in), (rows, rows_in), (vrows, vrows_in)]
        casts = [(selneg, selneg_in), (sel0, sel0_in), (sel1, sel1_in)]
        LOADED = 16 * (len(loads) + len(small))

        def full(t):
            return t[tuple(slice(None) for _ in t.shape)]

        stage_q = [probs[0:64, 0:2, :, :].rearrange("p a b c -> p (a b c)").rearrange("p (h d) -> p h d", h=HEADS),
                   V[0][0:64, :, :].rearrange("p a b -> p (a b)").rearrange("p (h d) -> p h d", h=HEADS)]
        stage_k = [probs[0:64, 2:4, :, :].rearrange("p a b c -> p (a b c)").rearrange("p (h d) -> p h d", h=HEADS),
                   V[1][0:64, :, :].rearrange("p a b -> p (a b)")[:, 0:HEADS * DC].rearrange("p (h d) -> p h d", h=HEADS)]
        A_WIDTH = (D, DC)

        def nth(signal, task, part=0):
            return counts.at[signal.name, task, part]

        def qk_tile(u, which, c):
            t = qk1[u % 2]
            return t[:, 2 * which + c // 2, (c % 2) * S:(c % 2 + 1) * S]

        with nc.Block() as block:
            @block.sync
            def _(sp):
                sp.dma_start(stage_q[0], wqT_sa).then_inc(w_a[0], 16)
                sp.dma_start(stage_k[0], wkT_sa).then_inc(w_a[0], 16)
                sp.dma_start(stage_q[1], wqT_ca).then_inc(w_a[1], 16)
                sp.dma_start(stage_k[1], wkT_ca).then_inc(w_a[1], 16)
                for dst, src in small:
                    sp.dma_start(full(dst), src).then_inc(w_rest, 16)

            @block.gpsimd
            def _(pool):
                nc.gpsimd.memset(half_neg[:, :], -0.5).then_inc(consts_set, 1)
                for i in range(2):
                    nc.gpsimd.memset(MT[i][:, :].bitcast(F32), 0.0).then_inc(consts_set, 1)
                for dst, src in casts:
                    pool.dma_start(full(dst), src).then_inc(w_cast, 16)
                pool.wait_ge(consts_set, 3)

            @block.tensor
            def _(pe):
                mm = nc.tensor.matmul
                for k in range(2):
                    pe.wait_ge(w_a[k], 32)
                    w = A_WIDTH[k]
                    for q in range(QUADS):
                        n = k * QUADS + q
                        if n >= 4:
                            pe.wait_ge(prep_lo, n - 3)
                        for j in range(4):
                            last = mm(banks[n % 4][:, j * w:(j + 1) * w], stage_q[k][:, 4 * q + j, :],
                                      stage_k[k][:, 4 * q + j, :], start=True, stop=True)
                        last.then_inc(prep_ready, 1)
                pe.wait_ge(prep_lo, 2 * QUADS)
                pe.wait_ge(w_rest, LOADED)
                pe.wait_ge(w_cast, 16 * len(casts))

            @block.scalar
            def _(act):
                for dst, src in loads:
                    act.dma_start(full(dst), src).then_inc(w_rest, 16)
                for k in range(2):
                    w = A_WIDTH[k]
                    for q in range(QUADS):
                        n = k * QUADS + q
                        act.wait_ge(prep_ready, n + 1)
                        nc.scalar.activation(A_hi[k][:, 4 * q:4 * q + 4, :].rearrange("p a b -> p (a b)"), banks[n % 4][:, 0:4 * w], ACT.Copy)\
                            .then_inc(prep_hi, 1)
                act.wait_ge(w_rest, LOADED)

            @block.vector
            def _(dve):
                tt_op = nc.vector.tensor_tensor
                for k in range(2):
                    w = A_WIDTH[k]
                    for q in range(QUADS):
                        n = k * QUADS + q
                        dve.wait_ge(prep_hi, n + 1)
                        tt_op(A_lo[k][:, 4 * q:4 * q + 4, :].rearrange("p a b -> p (a b)"), banks[n % 4][:, 0:4 * w],
                              A_hi[k][:, 4 * q:4 * q + 4, :].rearrange("p a b -> p (a b)").bitcast(F32), ALU.subtract).then_inc(prep_lo, 1)
                dve.wait_ge(w_rest, LOADED)

        with nc.Fori(0, ITERATIONS) as it:
            with nc.Block() as block:
                @block.sync
                def _(sp):
                    for s in range(STREAMS):
                        sp.dma_start(X[s][:, :, :], x_in[bass.ds(it * STREAMS + s, 1)].rearrange("o (t p) d -> p (o t) d", p=P)).then_inc(in_loaded, 16)
                        sp.dma_start(C[s][:, :, :], ctx_in[bass.ds(it * STREAMS + s, 1)].rearrange("o (t p) d -> p (o t) d", p=P)).then_inc(in_loaded, 16)
                    for s in range(STREAMS):
                        task = ("down", len(UNITS) - STREAMS + s, 0)
                        sp.wait_ge(out_ready, nth(out_ready, task))
                        sp.dma_start(out[bass.ds(it * STREAMS + s, 1)].rearrange("o (t p) d -> p (o t) d", p=P), XO[s][:, :, :]).then_inc(stored, 16)
                    sp.wait_ge(stored, 16 * STREAMS)

                @block.gpsimd
                def _(pool):
                    for task in tasks:
                        kind, u, i = task
                        if kind == "ln":
                            pool.wait_ge(mean_var, nth(mean_var, task))
                            nc.gpsimd.tensor_scalar(ve[:, :], mv[:, :, 1], EPS, None, ALU.add).then_inc(var_eps, 1)
                            pool.wait_ge(var_eps, nth(var_eps, task))
                            nc.gpsimd.tensor_tensor(rstd[:, :], ve[:, :], half_neg[:, :], ALU.pow).then_inc(rstd_ready, 1)
                        if kind == "scores" and i % TT == TT - 1:
                            t = i // TT
                            pool.wait_ge(probs_ready, nth(probs_ready, task))
                            if t >= 2:
                                pool.wait_ge(quad_done, nth(quad_done, ("pv", u, t // 2 - 1)))
                            elif u >= 1:
                                pool.wait_ge(quad_done, nth(quad_done, ("pv", u - 1, QUADS - 1)))
                            nc.gpsimd.tensor_tensor(psums[:, t % 2, :], probs[:, t % 4, 0, :], probs[:, t % 4, 1, :], ALU.add)\
                                .then_inc(presum, 1)

                @block.tensor
                def _(pe):
                    mm = nc.tensor.matmul
                    def side(task):
                        before = counts.before[task]
                        if before is not None:
                            freed = sems[release_of(before)]
                            pe.wait_ge(freed, nth(freed, before))
                        return side_bank[counts.bank[task]]

                    for n, task in enumerate(tasks):
                        kind, u, i = task
                        layer, cross, s = UNITS[u]
                        Kd = DC if cross else D
                        if kind == "ctx":
                            b = side(task)
                            pe.wait_ge(in_loaded, 16 * 2 * STREAMS)
                            for tt in range(TT):
                                last = nc.tensor.transpose(b[0:DC, tt * P:(tt + 1) * P], C[u][:, tt, :], ident[:, :])
                            last.then_inc(side_ready, 1)
                        elif kind == "ln":
                            b = side(task)
                            pe.wait_ge(z_ready, nth(z_ready, task))
                            for tt in range(TT):
                                last = nc.tensor.transpose(b[:, tt * P:(tt + 1) * P], z[:, tt, :], ident[:, :])
                            last.then_inc(side_ready, 1)
                        elif kind == "g":
                            b = side(task)
                            if i == 0:
                                pe.wait_ge(split_ready, nth(split_ready, ("ln", u, cross)))
                            for j in range(2):
                                h = 2 * i + j
                                o = b[0:Kd, j * S:(j + 1) * S]
                                mm(o, A_hi[cross][:, h, :], h_hi[s][:, :], start=True, stop=False)
                                mm(o, A_hi[cross][:, h, :], h_lo[s][:, :], start=False, stop=False)
                                last = mm(o, A_lo[cross][:, h, :], h_hi[s][:, :], start=False, stop=True)
                            last.then_inc(side_ready, 1)
                        elif kind == "qk":
                            b = side(task)
                            if i == 0:
                                pe.wait_ge(h32_ready, nth(h32_ready, ("ln", u, 3 + cross)))
                            for j in range(2):
                                c = 2 * (i % 2) + j
                                if i // 2 == 0:
                                    w, act = (wqk1[1] if cross else wqk1[0][:, 0, :]), h32
                                elif cross:
                                    w, act = wk1_cas, c32[s]
                                else:
                                    w, act = wqk1[0][:, 1, :], h32
                                last = mm(b[:, j * S:(j + 1) * S], w[:, c * P:(c + 1) * P], act[:, :], start=True, stop=True)
                            last.then_inc(side_ready, 1)
                        elif kind == "v":
                            b = side(task)
                            if i == 0:
                                pe.wait_ge(h32_ready, nth(h32_ready, ("ctx", s, 0) if cross else ("ln", u, layer * 3)))
                            tt, half = (i % 2, i // 2) if layer == 0 else (i, 0)
                            w = wv0[cross] if layer == 0 else wv1[cross]
                            act = c32[s] if cross else h32
                            last = mm(b[:, :], act[:, tt * P:(tt + 1) * P], w[:, half * 512:(half + 1) * 512], start=True, stop=True)
                            last.then_inc(side_ready, 1)
                        elif kind == "smax":
                            for par in range(2):
                                h = 2 * i + par
                                if i >= 1:
                                    pe.wait_ge(max_done, nth(max_done, ("smax", u, i - 1), par))
                                elif u >= 1:
                                    pe.wait_ge(max_done, nth(max_done, ("smax", u - 1, PAIRS - 1), par))
                                if par == 0:
                                    if layer == 0:
                                        pe.wait_ge(g_lo_ready, nth(g_lo_ready, ("g", u, i)))
                                    elif i == 0:
                                        pe.wait_ge(qk_ready, nth(qk_ready, ("qk", u, 3)))
                                for qt in range(TT):
                                    o = max_bank[par][:, qt * S:(qt + 1) * S]
                                    if layer == 0:
                                        q0 = par * S + qt * P
                                        last = mm(o, g_hi[0:Kd, i, q0:q0 + P], (c_hi if cross else h_hi)[s][:, :], start=True, stop=True)
                                    else:
                                        c, r = h % 4, SLOT * (h // 4)
                                        last = mm(o, qk_tile(u, 0, c)[r:r + SLOT, qt * P:(qt + 1) * P],
                                                  qk_tile(u, 1, c)[r:r + SLOT, :], start=True, stop=True, tile_position=(r, 0))
                                last.then_inc(smax_ready, 1)
                        elif kind == "mt":
                            b = side(task)
                            pe.wait_ge(max_parts, nth(max_parts, task))
                            for par in range(2):
                                for qt in range(TT):
                                    last = nc.tensor.transpose(b[0:2 * PAIRS, par * S + qt * P:par * S + (qt + 1) * P],
                                                               mx_parts[:, qt, par, :, :].rearrange("p a b -> p (a b)"), ident[:, :])
                            last.then_inc(side_ready, 1)
                        elif kind == "scores":
                            t, kb = divmod(i, TT)
                            if i == 0:
                                pe.wait_ge(mt_ready, nth(mt_ready, ("mt", u, 0)))
                            if t >= 1:
                                pe.wait_ge(probs_ready, nth(probs_ready, ("scores", u, i - TT)))
                            elif u >= 1:
                                pe.wait_ge(probs_ready, nth(probs_ready, ("scores", u - 1, TT * (PAIRS - 1) + kb)))
                            o = score_bank[kb]
                            ks = slice(kb * P, (kb + 1) * P)
                            mm(o[:, :], selneg[:, t, :], MT[u % 2][:, :], start=True, stop=(layer == 1))
                            if layer == 0:
                                k_hi, k_lo = (c_hi, c_lo) if cross else (h_hi, h_lo)
                                mm(o[:, :], k_hi[s][:, ks], g_hi[0:Kd, t, :], start=False, stop=False)
                                mm(o[:, :], k_hi[s][:, ks], g_lo[0:Kd, t, :], start=False, stop=False)
                                last = mm(o[:, :], k_lo[s][:, ks], g_hi[0:Kd, t, :], start=False, stop=True)
                            else:
                                for par in range(2):
                                    h = 2 * t + par
                                    c, r = h % 4, SLOT * (h // 4)
                                    last = mm(o[:, par * S:(par + 1) * S], qk_tile(u, 1, c)[r:r + SLOT, ks],
                                              qk_tile(u, 0, c)[r:r + SLOT, :], start=False, stop=True, tile_position=(r, 0),
                                              skip_group_check=True)
                            last.then_inc(scores_ready, 1)
                        elif kind == "pv":
                            pe.wait_ge(probs_ready, nth(probs_ready, ("scores", u, 2 * TT * (i + 1) - 1)))
                            if i >= 1:
                                pe.wait_ge(o_copied, nth(o_copied, ("pv", u, i - 1)))
                            elif u >= 1:
                                pe.wait_ge(o_copied, nth(o_copied, ("pv", u - 1, QUADS - 1)))
                            if i == 0:
                                for k in range(4 if layer == 0 else TT):
                                    values = v0_ready if layer == 0 else v1_ready
                                    pe.wait_ge(values, nth(values, ("v", u, k)))
                            if layer == 0:
                                for t in (2 * i, 2 * i + 1):
                                    for kb in range(TT):
                                        for par in range(2):
                                            h = 2 * t + par
                                            mm(pv_bank[64 * par:64 * par + 64, (t % 2) * S:(t % 2 + 1) * S],
                                               V[u % 2][:, kb, h * 64:(h + 1) * 64], probs[:, t % 4, kb, par * S:(par + 1) * S],
                                               start=(kb == 0), stop=(kb == TT - 1))
                            else:
                                for kb in range(TT):
                                    for j in range(4):
                                        h = 4 * i + j
                                        mm(pv_bank[SLOT * j:SLOT * (j + 1), 0:S], V[u % 2][:, kb, h * SLOT:(h + 1) * SLOT],
                                           probs[:, (h // 2) % 4, kb, (h % 2) * S:(h % 2 + 1) * S],
                                           start=(kb == 0), stop=(kb == TT - 1), tile_position=(0, SLOT * j))
                            pe.wait_ge(presum, nth(presum, ("scores", u, 2 * TT * (i + 1) - 1)))
                            if i == 0 and u >= 1:
                                pe.wait_ge(den_recip, nth(den_recip, ("rd", u - 1, 0)))
                            for j in range(4):
                                last = mm(den_bank[SLOT * j:SLOT * (j + 1), 0:S], e_cols[:, i, :],
                                          psums[:, j // 2, (j % 2) * S:(j % 2 + 1) * S],
                                          start=(i == 0), stop=(i == QUADS - 1), tile_position=(0, SLOT * j))
                            last.then_inc(quad_done, 1)
                        elif kind == "r":
                            b = side(task)
                            if i == 0:
                                pe.wait_ge(den_ready, nth(den_ready, ("rd", u, 0)))
                            for j in range(2):
                                w = (sel0 if layer == 0 else sel1)[:, 2 * i + j, :]
                                mm(b[:, j * S:(j + 1) * S], w, rd_hi[:, :], start=True, stop=False)
                                last = mm(b[:, j * S:(j + 1) * S], w, rd_lo[:, :], start=False, stop=True)
                            last.then_inc(side_ready, 1)
                        elif kind == "o":
                            b = side(task)
                            tiles = 8 if layer == 0 else 4
                            pe.wait_ge(o_scaled, nth(o_scaled, ("r", u, tiles // 2 - 1)))
                            w = wo0_s if layer == 0 else wo1_s
                            for tt in range(TT):
                                for k in range(tiles):
                                    last = mm(b[:, tt * D:(tt + 1) * D], o_un[:, k, tt * P:(tt + 1) * P], w[:, cross, k, :],
                                              start=(k == 0), stop=(k == tiles - 1))
                            last.then_inc(side_ready, 1)
                        elif kind == "up":
                            b = side(task)
                            if i == 0:
                                pe.wait_ge(h32_ready, nth(h32_ready, ("ln", u, layer * 3 + 2)))
                            for j in range(2):
                                c = (i + 4 * j) if layer == 0 else (2 * i + j)
                                w = w1_0s if layer == 0 else w1_1s
                                last = mm(b[:, j * S:(j + 1) * S], w[:, c * P:(c + 1) * P], h32[:, :], start=True, stop=True)
                            last.then_inc(side_ready, 1)
                        elif kind == "down":
                            b = side(task)
                            if layer == 0:
                                pe.wait_ge(act0_ready, nth(act0_ready, ("up", u, 3)))
                            else:
                                pe.wait_ge(act1_ready, nth(act1_ready, ("up", u, 1)))
                            w = w2_0s if layer == 0 else w2_1s
                            for tt in range(TT):
                                for k in range(4):
                                    last = mm(b[:, tt * D:(tt + 1) * D], hidden[:, k, tt * P:(tt + 1) * P], w[:, k, :],
                                              start=(k == 0), stop=(k == 3))
                            last.then_inc(side_ready, 1)

                @block.scalar
                def _(act):
                    for task in tasks:
                        kind, u, i = task
                        layer, cross, s = UNITS[u]
                        if kind in counts_side:
                            b = side_bank[counts.bank[task]]
                        if kind == "ctx":
                            act.wait_ge(side_ready, nth(side_ready, task))
                            nc.scalar.activation(c32[u][:, :], b[0:DC, 0:S], ACT.Copy).then_inc(h32_ready, 1)
                        elif kind == "ln":
                            act.wait_ge(side_ready, nth(side_ready, task))
                            nc.scalar.activation(h32[:, :], b[:, 0:S], ACT.Identity, scale=cols[:, LN_G + i:LN_G + i + 1],
                                                 bias=cols[:, LN_B + i:LN_B + i + 1]).then_inc(h32_ready, 1)
                        elif kind == "g":
                            Kd = DC if cross else D
                            act.wait_ge(side_ready, nth(side_ready, task))
                            nc.scalar.activation(g_hi[0:Kd, i, :], b[0:Kd, :], ACT.Copy).then_inc(g_hi_ready, 1)
                        elif kind == "qk":
                            act.wait_ge(side_ready, nth(side_ready, task))
                            for j in range(2):
                                k = QK_BM + (cross * 2 + i // 2) * 4 + 2 * (i % 2) + j
                                m = MASK + i // 2
                                last = nc.scalar.activation(qk_low[:, counts.bank[task], j, :].bitcast(F32R), b[:, j * S:(j + 1) * S], ACT.Identity,
                                                            scale=cols[:, m:m + 1], bias=cols[:, k:k + 1])
                            last.then_inc(qk_hi, 1)
                        elif kind == "v" and layer == 0:
                            act.wait_ge(side_ready, nth(side_ready, task))
                            tt, half = i % 2, i // 2
                            nc.scalar.activation(V[u % 2][:, tt, half * 512:(half + 1) * 512], b[:, :], ACT.Copy).then_inc(v0_ready, 1)
                        elif kind == "scores":
                            t, kb = divmod(i, TT)
                            act.wait_ge(scores_ready, nth(scores_ready, task))
                            nc.scalar.activation(probs[:, t % 4, kb, :], score_bank[kb][:, :], ACT.Exp, scale=EXP_SCALE[layer])\
                                .then_inc(probs_ready, 1)
                        elif kind == "pv":
                            act.wait_ge(quad_done, nth(quad_done, task))
                            if layer == 0:
                                dst = o_un[:, 2 * i:2 * i + 2, :].rearrange("p a b -> p (a b)")
                                nc.scalar.activation(dst, pv_bank[:, :], ACT.Copy).then_inc(o_copied, 1)
                            else:
                                nc.scalar.activation(o_un[:, i, :], pv_bank[:, 0:S], ACT.Copy).then_inc(o_copied, 1)
                        elif kind == "up":
                            act.wait_ge(side_ready, nth(side_ready, task))
                            if layer == 0:
                                k = FF_B1 + 4 + i
                                nc.scalar.activation(gate[:, counts.bank[task], :], b[:, S:2 * S], ACT.Gelu, bias=cols[:, k:k + 1])\
                                    .then_inc(gelu, 1)
                            else:
                                for j in range(2):
                                    k = MLP_B1 + 2 * i + j
                                    last = nc.scalar.activation(hidden[:, 2 * i + j, :], b[:, j * S:(j + 1) * S], ACT.Gelu, bias=cols[:, k:k + 1])
                                last.then_inc(act1_ready, 1)

                @block.vector
                def _(dve):
                    tt_op = nc.vector.tensor_tensor
                    for task in tasks:
                        kind, u, i = task
                        layer, cross, s = UNITS[u]
                        if kind in counts_side:
                            b = side_bank[counts.bank[task]]
                        if kind == "ctx":
                            dve.wait_ge(h32_ready, nth(h32_ready, task))
                            nc.vector.tensor_copy(c_hi[u][:, :], c32[u][:, :]).then_inc(split_hi, 1)
                            dve.wait_ge(split_hi, nth(split_hi, task))
                            tt_op(c_lo[u][:, :], c32[u][:, :], c_hi[u][:, :].bitcast(F32), ALU.subtract).then_inc(split_ready, 1)
                        elif kind == "ln":
                            if i == 0:
                                dve.wait_ge(in_loaded, 16 * 2 * STREAMS)
                            elif i == 3:
                                dve.wait_ge(x_ready, nth(x_ready, ("down", u - 2, 0)))
                            else:
                                dve.wait_ge(x_ready, nth(x_ready, ("o", u if i % 3 == 2 else u - 2, 0)))
                            for tt in range(TT):
                                last = nc.vector.bn_stats(stats[:, tt, :], X[s][:, tt, :])
                            last.then_inc(stats_done, 1)
                            dve.wait_ge(stats_done, nth(stats_done, task))
                            for tt in range(TT):
                                last = nc.vector.bn_aggr(mv[:, tt, :], stats[:, tt, :])
                            last.then_inc(mean_var, 1)
                            dve.wait_ge(rstd_ready, nth(rstd_ready, task))
                            for tt in range(TT):
                                last = nc.vector.tensor_scalar(z[:, tt, :], X[s][:, tt, :], mv[:, tt, 0:1], rstd[:, tt:tt + 1],
                                                               ALU.subtract, ALU.mult)
                            last.then_inc(z_ready, 1)
                            dve.wait_ge(z_ready, nth(z_ready, task))
                            tt_op(X[s][:, :, :], X[s][:, :, :], rows[:, i, :].unsqueeze(1).to_broadcast([P, TT, D]), ALU.add)\
                                .then_inc(x_bias, 1)
                            if i < 2:
                                dve.wait_ge(h32_ready, nth(h32_ready, task))
                                nc.vector.tensor_copy(h_hi[s][:, :], h32[:, :]).then_inc(split_hi, 1)
                                dve.wait_ge(split_hi, nth(split_hi, task))
                                tt_op(h_lo[s][:, :], h32[:, :], h_hi[s][:, :].bitcast(F32), ALU.subtract).then_inc(split_ready, 1)
                        elif kind == "g":
                            Kd = DC if cross else D
                            dve.wait_ge(g_hi_ready, nth(g_hi_ready, task))
                            tt_op(g_lo[0:Kd, i, :], b[0:Kd, :], g_hi[0:Kd, i, :].bitcast(F32), ALU.subtract).then_inc(g_lo_ready, 1)
                        elif kind == "qk":
                            dve.wait_ge(qk_hi, nth(qk_hi, task))
                            for j in range(2):
                                c = 2 * (i % 2) + j
                                k = QK_B + (cross * 2 + i // 2) * 4 + c
                                last = nc.vector.scalar_tensor_tensor(qk_tile(u, i // 2, c), b[:, j * S:(j + 1) * S], cols[:, k:k + 1],
                                                                      qk_low[:, counts.bank[task], j, :], ALU.add, ALU.subtract)
                            last.then_inc(qk_ready, 1)
                        elif kind == "v" and layer == 1:
                            dve.wait_ge(side_ready, nth(side_ready, task))
                            tt_op(V[u % 2][:, i, 0:512], b[:, :], vrows[:, cross, :], ALU.add).then_inc(v1_ready, 1)
                        elif kind == "smax":
                            for par in range(2):
                                dve.wait_ge(smax_ready, nth(smax_ready, task, par))
                                nc.vector.tensor_reduce(mx[:, :, par, i], max_bank[par][:, :].rearrange("p (a b) -> p a b", a=TT), AX.X, ALU.max)\
                                    .then_inc(max_done, 1)
                        elif kind == "mt":
                            dve.wait_ge(max_done, nth(max_done, ("smax", u, PAIRS - 1), 1))
                            nc.vector.tensor_copy(mx_hi[:, :, :, :], mx[:, :, :, :]).then_inc(max_hi, 1)
                            dve.wait_ge(max_hi, nth(max_hi, task))
                            nc.vector.tensor_copy(mx_parts[:, :, :, 0, :], mx_hi[:, :, :, :].bitcast(F32))
                            tt_op(mx_parts[:, :, :, 1, :], mx[:, :, :, :], mx_hi[:, :, :, :].bitcast(F32), ALU.subtract).then_inc(max_parts, 1)
                            dve.wait_ge(side_ready, nth(side_ready, task))
                            nc.vector.tensor_copy(MT[u % 2][0:2 * PAIRS, :], b[0:2 * PAIRS, :]).then_inc(mt_ready, 1)
                        elif kind == "rd":
                            dve.wait_ge(quad_done, nth(quad_done, ("pv", u, QUADS - 1)))
                            nc.vector.reciprocal(rd[:, :], den_bank[:, 0:S]).then_inc(den_recip, 1)
                            dve.wait_ge(den_recip, nth(den_recip, task))
                            nc.vector.tensor_copy(rd_hi[:, :], rd[:, :]).then_inc(den_hi, 1)
                            dve.wait_ge(den_hi, nth(den_hi, task))
                            tt_op(rd_lo[:, :], rd[:, :], rd_hi[:, :].bitcast(F32), ALU.subtract).then_inc(den_ready, 1)
                        elif kind == "r":
                            if i == 0:
                                dve.wait_ge(o_copied, nth(o_copied, ("pv", u, QUADS - 1)))
                            dve.wait_ge(side_ready, nth(side_ready, task))
                            o = o_un[:, 2 * i:2 * i + 2, :].rearrange("p a b -> p (a b)")
                            tt_op(o, b[:, :], o, ALU.mult).then_inc(o_scaled, 1)
                        elif kind in ("o", "down"):
                            k = layer * 3 + (cross if kind == "o" else 2)
                            dve.wait_ge(x_bias, nth(x_bias, ("ln", u, k)))
                            dve.wait_ge(side_ready, nth(side_ready, task))
                            y = b[:, 0:TT * D].rearrange("p (t d) -> p t d", t=TT)
                            if kind == "down" and layer == 1:
                                tt_op(XO[s][:, :, :], y, X[s][:, :, :], ALU.add).then_inc(out_ready, 1)
                            else:
                                tt_op(X[s][:, :, :], y, X[s][:, :, :], ALU.add).then_inc(x_ready, 1)
                        elif kind == "up" and layer == 0:
                            dve.wait_ge(gelu, nth(gelu, task))
                            k = FF_B1 + i
                            nc.vector.scalar_tensor_tensor(hidden[:, i, :], b[:, 0:S], cols[:, k:k + 1], gate[:, counts.bank[task], :],
                                                           ALU.add, ALU.mult).then_inc(act0_ready, 1)

            nc.all_engine_barrier(sems_to_clear=range(min(loop_sems), max(loop_sems) + 1))


counts_side = ("ctx", "ln", "g", "qk", "v", "mt", "r", "o", "up", "down")


def arrange(i):
    f = lambda name: np.asarray(i[name])
    heads_rows = lambda w, n: np.ascontiguousarray(w.T.reshape(HEADS, 64, n).transpose(1, 0, 2))
    a = {"x": f("x"), "ctx_768": f("ctx_768")}
    for k, n in (("sa", D), ("ca", DC)):
        a[f"wqT_{k}"] = heads_rows(f(f"L0_xattn_{k}_wq"), D)
        a[f"wkT_{k}"] = heads_rows(f(f"L0_xattn_{k}_wk"), n)
    a["wv0_sa"], a["wv0_ca"] = f("L0_xattn_sa_wv"), f("L0_xattn_ca_wv")
    a["wo0"] = np.stack([f(f"L0_xattn_{k}_wo").reshape(8, P, D) for k in ("sa", "ca")]).transpose(2, 0, 1, 3)
    a["w1_0"] = f("L0_xattn_ff_w1")
    a["w2_0"] = f("L0_xattn_ff_w2").reshape(4, P, D).transpose(1, 0, 2)
    order = [4 * r + c for c in range(4) for r in range(4)]
    slots = lambda w: np.repeat(w.reshape(HEADS, 1, 8, -1)[order], 4, axis=1).reshape(512, -1)
    pad = lambda w: np.concatenate([w.reshape(HEADS, 8, -1), np.zeros((HEADS, SLOT - 8, w.shape[-1] if w.ndim > 1 else 1), w.dtype)], 1).reshape(512, -1)
    q, k = [f(f"L1_xattn_sa_w{c}") for c in "qk"]
    a["wqk1_sa"] = np.stack([slots(q).T, slots(k).T], 1)
    a["wq1_ca"], a["wk1_ca"] = slots(f("L1_xattn_ca_wq")).T, slots(f("L1_xattn_ca_wk")).T
    a["wv1_sa"], a["wv1_ca"] = pad(f("L1_xattn_sa_wv")).T, pad(f("L1_xattn_ca_wv")).T
    a["wo1"] = np.stack([pad(f(f"L1_xattn_{c}_wo").T).reshape(4, P, D) for c in ("sa", "ca")]).transpose(2, 0, 1, 3)
    a["w1_1"] = f("L1_xattn_mlp_w1").T
    a["w2_1"] = f("L1_xattn_mlp_w2").T.reshape(4, P, D).transpose(1, 0, 2)
    cols = np.zeros((P, N_COLS), np.float32)
    for layer in range(2):
        for n in range(3):
            cols[:, LN_G + layer * 3 + n] = f(f"L{layer}_xattn_ln{n + 1}_g")
            cols[:, LN_B + layer * 3 + n] = f(f"L{layer}_xattn_ln{n + 1}_b")
    cols[:, FF_B1:FF_B1 + 8] = f("L0_xattn_ff_b1").reshape(8, P).T
    cols[:, MLP_B1:MLP_B1 + 4] = f("L1_xattn_mlp_b1").reshape(4, P).T
    low = {"q": np.array([0, 0, 1, 1]), "k": np.array([0, 1, 0, 1])}
    for ci, c in enumerate(("sa", "ca")):
        for wi, w in enumerate("qk"):
            b = slots(f(f"L1_xattn_{c}_b{w}")).reshape(4, P).T
            is_low = np.repeat(np.tile(low[w], 4), 8) == 1
            n = (ci * 2 + wi) * 4
            cols[:, QK_B + n:QK_B + n + 4] = b
            cols[is_low, QK_BM + n:QK_BM + n + 4] = b[is_low]
            cols[is_low, MASK + wi] = 1
    a["cols"] = cols
    row_names = [f"L0_xattn_{n}" for n in ("sa_bo", "ca_bo", "ff_b2")] + [f"L1_xattn_{n}" for n in ("sa_bo", "ca_bo", "mlp_b2")]
    a["rows"] = np.broadcast_to(np.stack([f(n) for n in row_names]), (P, 6, D))
    a["vrows"] = np.broadcast_to(np.stack([pad(f(f"L1_xattn_{c}_bv"))[:, 0] for c in ("sa", "ca")]), (P, 2, 512))
    a["ident"] = np.eye(P, dtype=np.float32)
    selneg = np.zeros((P, PAIRS, P), np.float32)
    for t in range(PAIRS):
        selneg[[t, PAIRS + t], t] = -1
    e = np.zeros((P, QUADS, SLOT), np.float32)
    for q in range(QUADS):
        e[:, q, q] = 1
    e[:, 0, QUADS:] = 1
    sel0, sel1 = np.zeros((P, PAIRS, P), np.float32), np.zeros((P, QUADS, P), np.float32)
    for t in range(PAIRS):
        for par in range(2):
            sel0[SLOT * (2 * (t % 2) + par) + t // 2, t, 64 * par:64 * par + 64] = 1
    for c in range(QUADS):
        for j in range(4):
            sel1[SLOT * j + c, c, SLOT * j:SLOT * (j + 1)] = 1
    a["selneg"], a["e"], a["sel0"], a["sel1"] = selneg, e, sel0, sel1
    return a


def kernel(**inputs):
    import concourse.bacc as bacc
    from concourse.bass_utils import run_bass_kernel_spmd

    arrays = {f"in_{k}": np.ascontiguousarray(v) for k, v in arrange(inputs).items()}
    nc = bacc.Bacc("TRN2", target_bir_lowering=False, num_devices=1)
    args = [nc.dram_tensor(k, v.shape, mybir.dt.from_np(v.dtype), kind="ExternalInput").ap() for k, v in arrays.items()]
    out = nc.dram_tensor("out", (BATCHES, S, D), F32, kind="ExternalOutput").ap()
    build(nc, *args, out)
    r = run_bass_kernel_spmd(nc, [arrays], core_ids=[0])
    return r.results[0]["out"]
```

```python
from contextlib import ExitStack

import numpy as np
import concourse.bass as bass
from concourse import mybir

F32 = mybir.dt.float32
F32R = mybir.dt.float32r
ACT = mybir.ActivationFunctionType
ALU = mybir.AluOpType
AX = mybir.AxisListType

P = 128
BATCHES, S, D, DC = 4, 256, 128, 96
HEADS = 16
PAIRS = HEADS // 2
QUADS = HEADS // 4
HD = (64, 8)
SLOT = 32
DF = 512
TT = S // P
EPS = 1e-5
EXP_SCALE = (64 ** -0.5, 8 ** -0.5)

UNITS = [(layer, cross, s) for layer in (0, 1) for cross in (0, 1) for s in range(BATCHES)]
LAST_SCORES = TT * PAIRS - 1

LN_G, LN_B = 0, 6
FF_B1 = 12
MLP_B1 = 20
QK_B = 24
QK_BM = 40
MASK = 56
N_COLS = 58


def attention(u):
    tasks = []
    for t in range(PAIRS):
        tasks += [("scores", u, TT * t + kb) for kb in range(TT)]
        if t == 0 and u >= 1:
            tasks.append(("pv", u - 1, QUADS - 1))
        if t >= 2 and t % 2 == 0:
            tasks.append(("pv", u, t // 2 - 1))
    return tasks


def tail(u):
    layer, cross, _ = UNITS[u]
    tasks = [("rd", u, 0)] + [("r", u, i) for i in range(4 if layer == 0 else 2)] + [("o", u, 0)]
    if cross:
        tasks += [("ln", u, layer * 3 + 2)] + [("up", u, i) for i in range(4 if layer == 0 else 2)] + [("down", u, 0)]
    return tasks


def head(u):
    layer, cross, _ = UNITS[u]
    smax = [("smax", u, t) for t in range(PAIRS)]
    if layer == 1:
        return [("qk", u, i) for i in (0, 2, 1, 3)] + smax + [("mt", u, 0)]
    tasks = [("split", u, 0), ("g", u, 0)]
    for t in range(1, PAIRS):
        tasks += [("g", u, t), smax[t - 1]]
    return tasks + [smax[-1], ("mt", u, 0)]


def first_norm(u):
    layer, cross, _ = UNITS[u]
    return ("ln", u, 3 * layer + cross)


def values(u):
    return [("v", u, i) for i in range(4 if UNITS[u][0] == 0 else TT)]


ORDER = [
    "hhhhhhthhhthhthhhhhhhhhhtvhtttthvvvh",
    "mhmmmhmhmmhmhmmmhmhmmmhmhhhmhmhvmhhvhhhvvh",
    "mhmmtvhmmttmttmhthmmmhmhmhhhmmmhmhmhmhmmhhhvhvhvh",
    "mhmmtmhmhmttmtthhthmmmhmmhhmmhmhmmhhmhmmhvhhvhvvh",
    "mmmhmmthhmttmtthhthmmmhmhmmmhmhmhmhmmhhmhhvhhvvvh",
    "mmhmvthmmthmtmtthhthmmmmhmhmhmhmhhmmhhmmmhvhhvhvh",
    "mmmhmtmhhmttmtthhtvmtmhmhtmhmmmmhmhhmtmththmhmhhthhvvvh",
    "mmmmhthmmtttmthhtmmtmmhmhhtmhttmhmhhmtmhhmmhmhhthvvhvvh",
    "mmmmmtvmttttmtmmtmhhmhhmthtmhththmhmhvhthmmhmmhm",
    "mhhmmthhthmthmhhtmthvvhtmmmmthmmhmhmmmmhttmttmmt",
    "hmhmmmmthhmmmhmmhtmmhvthmhmhvhthmmhmmmmh",
    "mmhhmtmmhhmmmhmthmmhmhvhmhtvhthmmmhmmmhm",
    "mhhmmthmmhmtmhvhmhvmhmmhmthmhmhmhmmmmmht",
    "mhhmmthmhmmmtthmhmmhmhmhvhmhvhtmmhmmmhmm",
    "hhmmhhmtmmhmmvmhmttmmhthmvhmhmmhmmmthmthtmht",
    "hhmmhhmmtmvmhmmtmhmmhmthmmmhtmmmmmthvhththt",
    "mmmmmmmttmtmmtmmmmmtmmttmmmt",
    "ttttttttt",
]


def strands(p):
    n = len(UNITS)
    main = attention(p) if 0 <= p < n else []
    behind, ahead, val = [], [], []
    if p == -1:
        behind = [("prep", 1, q) for q in range(QUADS)] + [("ctx", s, 0) for s in range(BATCHES)]
        ahead = [("prep", 0, q) for q in range(QUADS)] + [first_norm(0)]
    if p == n:
        behind += [("pv", p - 1, QUADS - 1)]
    if p >= 1:
        behind += tail(p - 1)
    if p + 1 < n:
        ahead += head(p + 1)
        if p + 2 < n:
            ahead.append(first_norm(p + 2))
        val = values(p + 1)
    return {"m": main, "t": behind, "h": ahead, "v": val}


def plan():
    tasks = []
    for p, order in zip(range(-1, len(UNITS) + 1), ORDER, strict=True):
        left = strands(p)
        for c in order:
            tasks.append(left[c].pop(0))
        assert not any(left.values())
    return tasks


def earlier(u):
    return max(n for n in range(u) if UNITS[n][2] == UNITS[u][2])


def signals_of(task):
    kind, u, i = task
    layer, cross, _ = UNITS[u]
    if kind == "prep":
        return [("side_ready", 0), ("a_hi_ready", 0), ("a_lo_ready", 0)]
    if kind == "ctx":
        return [("side_ready", 0), ("h32_ready", 0)]
    if kind == "ln":
        return [("stats_done", 0), ("mean_var", 0), ("var_eps", 0), ("rstd_ready", 0), ("z_ready", 0), ("x_bias", 0), ("side_ready", 0), ("h32_ready", 0)]
    if kind == "split":
        return [("split_hi", 0), ("split_ready", 0)]
    return {
        "g": [("side_ready", 0), ("g_hi_ready", 0), ("g_lo_ready", 0)],
        "qk": [("side_ready", 0), ("qk_hi", 0), ("qk_ready", 0)],
        "v": [("side_ready", 0), ("v0_ready" if layer == 0 else "v1_ready", 0)],
        "smax": [("smax_ready", 0), ("smax_ready", 1), ("max_done", 0), ("max_done", 1)],
        "mt": [("max_hi", 0), ("max_parts", 0), ("side_ready", 0), ("mt_ready", 0)],
        "scores": [("scores_ready", 0), ("probs_ready", 0)] + [("presum", 0)] * (i % TT == TT - 1),
        "pv": [("quad_done", 0), ("o_copied", 0)],
        "rd": [("den_recip", 0), ("den_hi", 0), ("den_ready", 0)],
        "r": [("side_ready", 0), ("o_scaled", 0)],
        "o": [("side_ready", 0), ("x_ready", 0)],
        "up": [("side_ready", 0)] + ([("gelu", 0), ("act0_ready", 0)] if layer == 0 else [("act1_ready", 0)]),
        "down": [("side_ready", 0)] + ([("x_ready", 0)] if layer == 0 else [("out_ready", 0)]),
    }[kind]


RELEASE = {"prep": "a_lo_ready", "ctx": "h32_ready", "ln": "h32_ready", "g": "g_lo_ready", "qk": "qk_ready", "mt": "mt_ready", "r": "o_scaled", "o": "x_ready"}


def release_of(task):
    kind, u, i = task
    layer = UNITS[u][0]
    if kind == "v":
        return "v0_ready" if layer == 0 else "v1_ready"
    if kind == "up":
        return "act0_ready" if layer == 0 else "act1_ready"
    if kind == "down":
        return "x_ready" if layer == 0 else "out_ready"
    return RELEASE[kind]


class Counts:

    def __init__(self, tasks):
        self.at, self.total, self.bank, self.before = {}, {}, {}, {}
        sides = []
        for task in tasks:
            for sig, part in signals_of(task):
                self.total[sig] = self.total.get(sig, 0) + 1
                self.at[sig, task, part] = self.total[sig]
                if sig == "side_ready":
                    self.bank[task] = len(sides) % 2
                    self.before[task] = sides[-2] if len(sides) >= 2 else None
                    sides.append(task)


def build(nc, x_in, ctx_in, wqT_sa, wkT_sa, wqT_ca, wkT_ca, wv0_sa, wv0_ca, wo0, w1_0, w2_0,
          wqk1_sa, wq1_ca, wk1_ca, wv1_sa, wv1_ca, wo1, w1_1, w2_1, cols_in, rows_in, vrows_in,
          ident_in, selneg_in, e_in, sel0_in, sel1_in, out):
    tasks = plan()
    counts = Counts(tasks)
    with ExitStack() as ctx:
        def sb(name, shape, dt=F32):
            return ctx.enter_context(nc.sbuf_tensor(name, shape, dt))

        A_hi = [sb("A_hi_sa", [P, HEADS, D], F32R), sb("A_hi_ca", [P, HEADS, DC], F32R)]
        A_lo = [sb("A_lo_sa", [P, HEADS, D], F32R), sb("A_lo_ca", [P, HEADS, DC], F32R)]
        wv0 = [sb("wv0_sa_s", [P, 1024]), sb("wv0_ca_s", [DC, 1024])]
        wo0_s = sb("wo0_s", [P, 2, 8, D])
        w1_0s = sb("w1_0s", [P, 2 * DF])
        w2_0s = sb("w2_0s", [P, 4, D])
        wqk1 = [sb("wqk1_sa_s", [P, 2, 512]), sb("wq1_ca_s", [P, 512])]
        wk1_cas = sb("wk1_ca_s", [DC, 512])
        wv1 = [sb("wv1_sa_s", [P, 512]), sb("wv1_ca_s", [DC, 512])]
        wo1_s = sb("wo1_s", [P, 2, 4, D])
        w1_1s = sb("w1_1s", [P, DF])
        w2_1s = sb("w2_1s", [P, 4, D])
        cols = sb("cols", [P, N_COLS])
        rows = sb("rows", [P, 6, D])
        vrows = sb("vrows", [P, 2, 512])
        ident = sb("ident", [P, P])
        selneg = sb("selneg", [P, PAIRS, P], F32R)
        e_cols = sb("e_cols", [P, QUADS, SLOT])
        sel0 = sb("sel0", [P, PAIRS, P], F32R)
        sel1 = sb("sel1", [P, QUADS, P], F32R)
        half_neg = sb("half_neg", [P, TT])

        X = [sb(f"x{s}", [P, TT, D]) for s in range(BATCHES)]
        c32 = [sb(f"c32_{s}", [DC, S]) for s in range(BATCHES)]

        h_hi = [sb(f"h_hi{i}", [P, S], F32R) for i in range(2)]
        h_lo = [sb(f"h_lo{i}", [P, S], F32R) for i in range(2)]
        c_hi = [sb(f"c_hi{i}", [DC, S], F32R) for i in range(2)]
        c_lo = [sb(f"c_lo{i}", [DC, S], F32R) for i in range(2)]

        stats = sb("stats", [P, 2, TT, 6])
        mv = sb("mv", [P, 2, TT, 2])
        ve = sb("ve", [P, 2, TT])
        rstd = sb("rstd", [P, 2, TT])
        z = sb("z", [P, 2, TT, D])
        h32 = sb("h32", [P, 2, S])

        g_hi = sb("g_hi", [P, PAIRS, 2 * S], F32R)
        g_lo = sb("g_lo", [P, PAIRS, 2 * S], F32R)
        qk1 = [g_hi, g_lo]
        V = [sb(f"v{i}", [P, TT, 1024]) for i in range(2)]
        probs = sb("probs", [P, 4, TT, 2 * S])
        psums = sb("psums", [P, 4, 2 * S])
        o_un = sb("o_un", [P, PAIRS, S])
        rd = sb("rd", [P, S])
        rd_hi = sb("rd_hi", [P, S], F32R)
        rd_lo = sb("rd_lo", [P, S], F32R)
        mx = sb("mx", [P, TT, 2, PAIRS])
        mx_hi = sb("mx_hi", [P, TT, 2, PAIRS], F32R)
        mx_parts = sb("mx_parts", [P, TT, 2, 2, PAIRS])
        MT = [sb(f"mt{i}", [P, 2 * S], F32R) for i in range(2)]
        qk_low = sb("qk_low", [P, 2, 2, S])
        gate = sb("gate", [P, 2, S])
        hidden = sb("hidden", [P, 4, S])
        C = [hidden[:, s, 0:TT * DC].rearrange("p (t d) -> p t d", t=TT) for s in range(BATCHES)]

        banks = [ctx.enter_context(nc.psum_tensor(f"bank{i}", [P, 512], F32)) for i in range(8)]
        max_bank = banks[0:2]
        score_bank = banks[2:4]
        pv_bank = banks[4]
        den_bank = banks[6]
        side_bank = [banks[5], banks[7]]

        sem = lambda name: ctx.enter_context(nc.semaphore(name))
        side_ready, smax_ready, scores_ready, quad_done = sem("side_ready"), sem("smax_ready"), sem("scores_ready"), sem("quad_done")
        stats_done, mean_var, var_eps, rstd_ready = sem("stats_done"), sem("mean_var"), sem("var_eps"), sem("rstd_ready")
        z_ready, h32_ready, split_hi, split_ready = sem("z_ready"), sem("h32_ready"), sem("split_hi"), sem("split_ready")
        a_hi_ready, a_lo_ready = sem("a_hi_ready"), sem("a_lo_ready")
        g_hi_ready, g_lo_ready, qk_hi, qk_ready = sem("g_hi_ready"), sem("g_lo_ready"), sem("qk_hi"), sem("qk_ready")
        v0_ready, v1_ready = sem("v0_ready"), sem("v1_ready")
        max_done, max_hi, max_parts, mt_ready = sem("max_done"), sem("max_hi"), sem("max_parts"), sem("mt_ready")
        probs_ready, presum, o_copied = sem("probs_ready"), sem("presum"), sem("o_copied")
        den_recip, den_hi, den_ready, o_scaled = sem("den_recip"), sem("den_hi"), sem("den_ready"), sem("o_scaled")
        x_bias, x_ready, out_ready = sem("x_bias"), sem("x_ready"), sem("out_ready")
        gelu, act0_ready, act1_ready = sem("gelu"), sem("act0_ready"), sem("act1_ready")
        sems = {x.name: x for x in (
            side_ready, smax_ready, scores_ready, quad_done, stats_done, mean_var, var_eps, rstd_ready, z_ready, h32_ready,
            split_hi, split_ready, g_hi_ready, g_lo_ready, qk_hi, qk_ready, v0_ready, v1_ready, max_done, max_hi, max_parts,
            mt_ready, probs_ready, presum, o_copied, den_recip, den_hi, den_ready, o_scaled, x_bias, x_ready, out_ready,
            gelu, act0_ready, act1_ready, a_hi_ready, a_lo_ready)}
        assert set(counts.total) == set(sems)
        x_loaded = [sem(f"x{s}_loaded") for s in range(BATCHES)]
        c_loaded = sem("contexts_loaded")
        stored = sem("stored")
        w_a = [sem("wqk_sa_loaded"), sem("wqk_ca_loaded")]
        consts_loaded, selectors_loaded = sem("consts_loaded"), sem("selectors_loaded")
        consts_set = sem("consts_set")

        consts = [(ident, ident_in), (cols, cols_in), (rows, rows_in), (e_cols, e_in), (vrows, vrows_in)]
        weights = {
            "wv0": [(wv0[0], wv0_sa), (wv0[1], wv0_ca)],
            "rest0": [(wo0_s, wo0), (w1_0s, w1_0), (w2_0s, w2_0)],
            "qkv1": [(wqk1[0], wqk1_sa), (wqk1[1], wq1_ca), (wk1_cas, wk1_ca), (wv1[0], wv1_sa), (wv1[1], wv1_ca)],
            "rest1": [(wo1_s, wo1), (w1_1s, w1_1), (w2_1s, w2_1)],
        }
        w_loaded = {k: sem(f"{k}_loaded") for k in weights}
        casts = [(selneg, selneg_in), (sel0, sel0_in), (sel1, sel1_in)]

        def full(t):
            return t[tuple(slice(None) for _ in t.shape)]

        stage_q = [probs[0:64, 0:2, :, :].rearrange("p a b c -> p (a b c)").rearrange("p (h d) -> p h d", h=HEADS),
                   o_un[0:64, :, :].rearrange("p a b -> p (a b)").rearrange("p (h d) -> p h d", h=HEADS)]
        stage_k = [probs[0:64, 2:4, :, :].rearrange("p a b c -> p (a b c)").rearrange("p (h d) -> p h d", h=HEADS),
                   V[1][0:64, :, :].rearrange("p a b -> p (a b)")[:, 0:HEADS * DC].rearrange("p (h d) -> p h d", h=HEADS)]
        A_WIDTH = (D, DC)

        def nth(signal, task, part=0):
            return counts.at[signal.name, task, part]

        def qk_tile(u, which, c):
            t = qk1[u % 2]
            return t[:, 2 * which + c // 2, (c % 2) * S:(c % 2 + 1) * S]

        def o_tile(u, k):
            return k + (4 * (u % 2) if UNITS[u][0] == 1 else 0)

        def norm(task):
            return int(task[2] % 3 == 2)

        with nc.Block() as block:
            @block.sync
            def _(sp):
                sp.dma_start(stage_q[0], wqT_sa).then_inc(w_a[0], 16)
                sp.dma_start(X[0][:, :, :], x_in[0].rearrange("(t p) d -> p t d", p=P)).then_inc(x_loaded[0], 16)
                sp.dma_start(stage_q[1], wqT_ca).then_inc(w_a[1], 16)
                for dst, src in weights["wv0"]:
                    sp.dma_start(full(dst), src).then_inc(w_loaded["wv0"], 16)
                for s in range(1, BATCHES):
                    sp.dma_start(X[s][:, :, :], x_in[s].rearrange("(t p) d -> p t d", p=P)).then_inc(x_loaded[s], 16)
                for k in ("rest0", "qkv1", "rest1"):
                    for dst, src in weights[k]:
                        sp.dma_start(full(dst), src).then_inc(w_loaded[k], 16)
                for s in range(BATCHES):
                    task = ("down", len(UNITS) - BATCHES + s, 0)
                    sp.wait_ge(out_ready, nth(out_ready, task))
                    sp.dma_start(out[s].rearrange("(t p) d -> p t d", p=P), X[s][:, :, :]).then_inc(stored, 16)
                sp.wait_ge(stored, 16 * BATCHES)

            @block.gpsimd
            def _(pool):
                nc.gpsimd.memset(half_neg[:, :], -0.5).then_inc(consts_set, 1)
                for i in range(2):
                    nc.gpsimd.memset(MT[i][:, :].bitcast(F32), 0.0).then_inc(consts_set, 1)
                for dst, src in casts:
                    pool.dma_start(full(dst), src).then_inc(selectors_loaded, 16)
                pool.wait_ge(consts_set, 3)
                for task in tasks:
                    kind, u, i = task
                    if kind == "ln":
                        n = norm(task)
                        pool.wait_ge(var_eps, nth(var_eps, task))
                        nc.gpsimd.tensor_tensor(rstd[:, n, :], ve[:, n, :], half_neg[:, :], ALU.pow).then_inc(rstd_ready, 1)
                    if kind == "scores" and i % TT == TT - 1:
                        t = i // TT
                        pool.wait_ge(probs_ready, nth(probs_ready, task))
                        if t >= 4:
                            pool.wait_ge(quad_done, nth(quad_done, ("pv", u, t // 2 - 2)))
                        elif u >= 1:
                            pool.wait_ge(quad_done, nth(quad_done, ("pv", u - 1, QUADS - 2 + t // 2)))
                        nc.gpsimd.tensor_tensor(psums[:, t % 4, :], probs[:, t % 4, 0, :], probs[:, t % 4, 1, :], ALU.add)\
                            .then_inc(presum, 1)

            @block.tensor
            def _(pe):
                mm = nc.tensor.matmul
                def side(task):
                    before = counts.before[task]
                    if before is not None:
                        freed = sems[release_of(before)]
                        pe.wait_ge(freed, nth(freed, before))
                    return side_bank[counts.bank[task]]

                for n, task in enumerate(tasks):
                    kind, u, i = task
                    layer, cross, s = UNITS[u]
                    Kd = DC if cross else D
                    if kind == "prep":
                        b = side(task)
                        w = A_WIDTH[u]
                        if i == 0:
                            pe.wait_ge(w_a[u], 32)
                        for j in range(4):
                            last = mm(b[:, j * w:(j + 1) * w], stage_q[u][:, 4 * i + j, :], stage_k[u][:, 4 * i + j, :],
                                      start=True, stop=True)
                        last.then_inc(side_ready, 1)
                    elif kind == "ctx":
                        b = side(task)
                        if u == 0:
                            pe.wait_ge(c_loaded, 16 * BATCHES)
                            pe.wait_ge(consts_loaded, 16 * len(consts))
                        for tt in range(TT):
                            last = nc.tensor.transpose(b[0:DC, tt * P:(tt + 1) * P], C[u][:, tt, :], ident[:, :])
                        last.then_inc(side_ready, 1)
                    elif kind == "ln":
                        b = side(task)
                        pe.wait_ge(z_ready, nth(z_ready, task))
                        if u == 0:
                            pe.wait_ge(consts_loaded, 16 * len(consts))
                        for tt in range(TT):
                            last = nc.tensor.transpose(b[:, tt * P:(tt + 1) * P], z[:, norm(task), tt, :], ident[:, :])
                        last.then_inc(side_ready, 1)
                    elif kind == "g":
                        b = side(task)
                        if i == 0:
                            pe.wait_ge(split_ready, nth(split_ready, ("split", u, 0)))
                        if u in (0, BATCHES) and i % 2 == 0:
                            pe.wait_ge(a_lo_ready, nth(a_lo_ready, ("prep", cross, i // 2)))
                        for j in range(2):
                            h = 2 * i + j
                            o = b[0:Kd, j * S:(j + 1) * S]
                            mm(o, A_hi[cross][:, h, :], h_hi[u % 2][:, :], start=True, stop=False)
                            mm(o, A_hi[cross][:, h, :], h_lo[u % 2][:, :], start=False, stop=False)
                            last = mm(o, A_lo[cross][:, h, :], h_hi[u % 2][:, :], start=False, stop=True)
                        last.then_inc(side_ready, 1)
                    elif kind == "qk":
                        b = side(task)
                        if i == 0:
                            pe.wait_ge(h32_ready, nth(h32_ready, ("ln", u, 3 + cross)))
                            if u == 2 * BATCHES:
                                pe.wait_ge(w_loaded["qkv1"], 16 * len(weights["qkv1"]))
                        for j in range(2):
                            c = 2 * (i % 2) + j
                            if i // 2 == 0:
                                w, act = (wqk1[1] if cross else wqk1[0][:, 0, :]), h32[:, 0, :]
                            elif cross:
                                w, act = wk1_cas, c32[s][:, :]
                            else:
                                w, act = wqk1[0][:, 1, :], h32[:, 0, :]
                            last = mm(b[:, j * S:(j + 1) * S], w[:, c * P:(c + 1) * P], act, start=True, stop=True)
                        last.then_inc(side_ready, 1)
                    elif kind == "v":
                        b = side(task)
                        if i == 0:
                            pe.wait_ge(h32_ready, nth(h32_ready, ("ctx", s, 0) if cross else ("ln", u, layer * 3)))
                        if u == 0 and i == 0:
                            pe.wait_ge(w_loaded["wv0"], 16 * len(weights["wv0"]))
                        if u == 2 * BATCHES and i == 0:
                            pe.wait_ge(w_loaded["qkv1"], 16 * len(weights["qkv1"]))
                        tt, half = (i % 2, i // 2) if layer == 0 else (i, 0)
                        w = wv0[cross] if layer == 0 else wv1[cross]
                        act = c32[s] if cross else h32[:, 0, :]
                        last = mm(b[:, :], act[:, tt * P:(tt + 1) * P], w[:, half * 512:(half + 1) * 512], start=True, stop=True)
                        last.then_inc(side_ready, 1)
                    elif kind == "smax":
                        for par in range(2):
                            h = 2 * i + par
                            if i >= 1:
                                pe.wait_ge(max_done, nth(max_done, ("smax", u, i - 1), par))
                            elif u >= 1:
                                pe.wait_ge(max_done, nth(max_done, ("smax", u - 1, PAIRS - 1), par))
                            if par == 0:
                                if layer == 0:
                                    pe.wait_ge(g_lo_ready, nth(g_lo_ready, ("g", u, i)))
                                elif i == 0:
                                    pe.wait_ge(qk_ready, nth(qk_ready, ("qk", u, 3)))
                            for qt in range(TT):
                                o = max_bank[par][:, qt * S:(qt + 1) * S]
                                if layer == 0:
                                    q0 = par * S + qt * P
                                    last = mm(o, g_hi[0:Kd, i, q0:q0 + P], (c_hi if cross else h_hi)[u % 2][:, :], start=True, stop=True)
                                else:
                                    c, r = h % 4, SLOT * (h // 4)
                                    last = mm(o, qk_tile(u, 0, c)[r:r + SLOT, qt * P:(qt + 1) * P],
                                              qk_tile(u, 1, c)[r:r + SLOT, :], start=True, stop=True, tile_position=(r, 0))
                            last.then_inc(smax_ready, 1)
                    elif kind == "mt":
                        b = side(task)
                        pe.wait_ge(max_parts, nth(max_parts, task))
                        for par in range(2):
                            for qt in range(TT):
                                last = nc.tensor.transpose(b[0:2 * PAIRS, par * S + qt * P:par * S + (qt + 1) * P],
                                                           mx_parts[:, qt, par, :, :].rearrange("p a b -> p (a b)"), ident[:, :])
                        last.then_inc(side_ready, 1)
                    elif kind == "scores":
                        t, kb = divmod(i, TT)
                        if i == 0:
                            pe.wait_ge(mt_ready, nth(mt_ready, ("mt", u, 0)))
                        if i == 0 and u == 0:
                            pe.wait_ge(selectors_loaded, 16 * len(casts))
                            pe.wait_ge(consts_set, 3)
                        if t >= 1:
                            pe.wait_ge(probs_ready, nth(probs_ready, ("scores", u, i - TT)))
                        elif u >= 1:
                            pe.wait_ge(probs_ready, nth(probs_ready, ("scores", u - 1, TT * (PAIRS - 1) + kb)))
                        o = score_bank[kb]
                        ks = slice(kb * P, (kb + 1) * P)
                        mm(o[:, :], selneg[:, t, :], MT[u % 2][:, :], start=True, stop=(layer == 1))
                        if layer == 0:
                            k_hi, k_lo = (c_hi, c_lo) if cross else (h_hi, h_lo)
                            mm(o[:, :], k_hi[u % 2][:, ks], g_hi[0:Kd, t, :], start=False, stop=False)
                            mm(o[:, :], k_hi[u % 2][:, ks], g_lo[0:Kd, t, :], start=False, stop=False)
                            last = mm(o[:, :], k_lo[u % 2][:, ks], g_hi[0:Kd, t, :], start=False, stop=True)
                        else:
                            for par in range(2):
                                h = 2 * t + par
                                c, r = h % 4, SLOT * (h // 4)
                                last = mm(o[:, par * S:(par + 1) * S], qk_tile(u, 1, c)[r:r + SLOT, ks],
                                          qk_tile(u, 0, c)[r:r + SLOT, :], start=False, stop=True, tile_position=(r, 0),
                                          skip_group_check=True)
                        last.then_inc(scores_ready, 1)
                    elif kind == "pv":
                        pe.wait_ge(probs_ready, nth(probs_ready, ("scores", u, 2 * TT * (i + 1) - 1)))
                        if i >= 1:
                            pe.wait_ge(o_copied, nth(o_copied, ("pv", u, i - 1)))
                        elif u >= 1:
                            pe.wait_ge(o_copied, nth(o_copied, ("pv", u - 1, QUADS - 1)))
                        if i == 0:
                            for k in range(4 if layer == 0 else TT):
                                values = v0_ready if layer == 0 else v1_ready
                                pe.wait_ge(values, nth(values, ("v", u, k)))
                        if layer == 0:
                            for t in (2 * i, 2 * i + 1):
                                for kb in range(TT):
                                    for par in range(2):
                                        h = 2 * t + par
                                        mm(pv_bank[64 * par:64 * par + 64, (t % 2) * S:(t % 2 + 1) * S],
                                           V[u % 2][:, kb, h * 64:(h + 1) * 64], probs[:, t % 4, kb, par * S:(par + 1) * S],
                                           start=(kb == 0), stop=(kb == TT - 1))
                        else:
                            for kb in range(TT):
                                for j in range(4):
                                    h = 4 * i + j
                                    mm(pv_bank[SLOT * j:SLOT * (j + 1), 0:S], V[u % 2][:, kb, h * SLOT:(h + 1) * SLOT],
                                       probs[:, (h // 2) % 4, kb, (h % 2) * S:(h % 2 + 1) * S],
                                       start=(kb == 0), stop=(kb == TT - 1), tile_position=(0, SLOT * j))
                        pe.wait_ge(presum, nth(presum, ("scores", u, 2 * TT * (i + 1) - 1)))
                        if i == 0 and u >= 1:
                            pe.wait_ge(den_recip, nth(den_recip, ("rd", u - 1, 0)))
                        for j in range(4):
                            last = mm(den_bank[SLOT * j:SLOT * (j + 1), 0:S], e_cols[:, i, :],
                                      psums[:, (2 * i + j // 2) % 4, (j % 2) * S:(j % 2 + 1) * S],
                                      start=(i == 0), stop=(i == QUADS - 1), tile_position=(0, SLOT * j))
                        last.then_inc(quad_done, 1)
                    elif kind == "r":
                        b = side(task)
                        if i == 0:
                            pe.wait_ge(den_ready, nth(den_ready, ("rd", u, 0)))
                        for j in range(2):
                            w = (sel0 if layer == 0 else sel1)[:, 2 * i + j, :]
                            mm(b[:, j * S:(j + 1) * S], w, rd_hi[:, :], start=True, stop=False)
                            last = mm(b[:, j * S:(j + 1) * S], w, rd_lo[:, :], start=False, stop=True)
                        last.then_inc(side_ready, 1)
                    elif kind == "o":
                        b = side(task)
                        tiles = 8 if layer == 0 else 4
                        pe.wait_ge(o_scaled, nth(o_scaled, ("r", u, tiles // 2 - 1)))
                        w = wo0_s if layer == 0 else wo1_s
                        if u in (0, 2 * BATCHES):
                            group = "rest0" if layer == 0 else "rest1"
                            pe.wait_ge(w_loaded[group], 16 * len(weights[group]))
                        for tt in range(TT):
                            for k in range(tiles):
                                last = mm(b[:, tt * D:(tt + 1) * D], o_un[:, o_tile(u, k), tt * P:(tt + 1) * P], w[:, cross, k, :],
                                          start=(k == 0), stop=(k == tiles - 1))
                        last.then_inc(side_ready, 1)
                    elif kind == "up":
                        b = side(task)
                        if i == 0:
                            pe.wait_ge(h32_ready, nth(h32_ready, ("ln", u, layer * 3 + 2)))
                        for j in range(2):
                            c = (i + 4 * j) if layer == 0 else (2 * i + j)
                            w = w1_0s if layer == 0 else w1_1s
                            last = mm(b[:, j * S:(j + 1) * S], w[:, c * P:(c + 1) * P], h32[:, 1, :], start=True, stop=True)
                        last.then_inc(side_ready, 1)
                    elif kind == "down":
                        b = side(task)
                        if layer == 0:
                            pe.wait_ge(act0_ready, nth(act0_ready, ("up", u, 3)))
                        else:
                            pe.wait_ge(act1_ready, nth(act1_ready, ("up", u, 1)))
                        w = w2_0s if layer == 0 else w2_1s
                        for tt in range(TT):
                            for k in range(4):
                                last = mm(b[:, tt * D:(tt + 1) * D], hidden[:, k, tt * P:(tt + 1) * P], w[:, k, :],
                                          start=(k == 0), stop=(k == 3))
                        last.then_inc(side_ready, 1)

            @block.scalar
            def _(act):
                act.dma_start(stage_k[0], wkT_sa).then_inc(w_a[0], 16)
                for dst, src in consts:
                    act.dma_start(full(dst), src).then_inc(consts_loaded, 16)
                act.dma_start(stage_k[1], wkT_ca).then_inc(w_a[1], 16)
                for s in range(BATCHES):
                    act.dma_start(C[s], ctx_in[s].rearrange("(t p) d -> p t d", p=P)).then_inc(c_loaded, 16)
                for task in tasks:
                    kind, u, i = task
                    layer, cross, s = UNITS[u]
                    if kind in counts_side:
                        b = side_bank[counts.bank[task]]
                    if kind == "prep":
                        w = A_WIDTH[u]
                        act.wait_ge(side_ready, nth(side_ready, task))
                        nc.scalar.activation(A_hi[u][:, 4 * i:4 * i + 4, :].rearrange("p a b -> p (a b)"), b[:, 0:4 * w], ACT.Copy)\
                            .then_inc(a_hi_ready, 1)
                    elif kind == "ctx":
                        act.wait_ge(side_ready, nth(side_ready, task))
                        nc.scalar.activation(c32[u][:, :], b[0:DC, 0:S], ACT.Copy).then_inc(h32_ready, 1)
                    elif kind == "ln":
                        if u == 0:
                            act.wait_ge(consts_loaded, 16 * len(consts))
                        act.wait_ge(side_ready, nth(side_ready, task))
                        nc.scalar.activation(h32[:, norm(task), :], b[:, 0:S], ACT.Identity, scale=cols[:, LN_G + i:LN_G + i + 1],
                                             bias=cols[:, LN_B + i:LN_B + i + 1]).then_inc(h32_ready, 1)
                    elif kind == "g":
                        Kd = DC if cross else D
                        act.wait_ge(side_ready, nth(side_ready, task))
                        nc.scalar.activation(g_hi[0:Kd, i, :], b[0:Kd, :], ACT.Copy).then_inc(g_hi_ready, 1)
                    elif kind == "qk":
                        act.wait_ge(side_ready, nth(side_ready, task))
                        for j in range(2):
                            k = QK_BM + (cross * 2 + i // 2) * 4 + 2 * (i % 2) + j
                            m = MASK + i // 2
                            last = nc.scalar.activation(qk_low[:, counts.bank[task], j, :].bitcast(F32R), b[:, j * S:(j + 1) * S], ACT.Identity,
                                                        scale=cols[:, m:m + 1], bias=cols[:, k:k + 1])
                        last.then_inc(qk_hi, 1)
                    elif kind == "v" and layer == 0:
                        act.wait_ge(side_ready, nth(side_ready, task))
                        tt, half = i % 2, i // 2
                        nc.scalar.activation(V[u % 2][:, tt, half * 512:(half + 1) * 512], b[:, :], ACT.Copy).then_inc(v0_ready, 1)
                    elif kind == "scores":
                        t, kb = divmod(i, TT)
                        act.wait_ge(scores_ready, nth(scores_ready, task))
                        nc.scalar.activation(probs[:, t % 4, kb, :], score_bank[kb][:, :], ACT.Exp, scale=EXP_SCALE[layer])\
                            .then_inc(probs_ready, 1)
                    elif kind == "pv":
                        act.wait_ge(quad_done, nth(quad_done, task))
                        if layer == 0:
                            dst = o_un[:, 2 * i:2 * i + 2, :].rearrange("p a b -> p (a b)")
                            nc.scalar.activation(dst, pv_bank[:, :], ACT.Copy).then_inc(o_copied, 1)
                        else:
                            nc.scalar.activation(o_un[:, o_tile(u, i), :], pv_bank[:, 0:S], ACT.Copy).then_inc(o_copied, 1)
                    elif kind == "up":
                        act.wait_ge(side_ready, nth(side_ready, task))
                        if layer == 0:
                            k = FF_B1 + 4 + i
                            nc.scalar.activation(gate[:, counts.bank[task], :], b[:, S:2 * S], ACT.Gelu, bias=cols[:, k:k + 1])\
                                .then_inc(gelu, 1)
                        else:
                            for j in range(2):
                                k = MLP_B1 + 2 * i + j
                                last = nc.scalar.activation(hidden[:, 2 * i + j, :], b[:, j * S:(j + 1) * S], ACT.Gelu, bias=cols[:, k:k + 1])
                            last.then_inc(act1_ready, 1)

            @block.vector
            def _(dve):
                tt_op = nc.vector.tensor_tensor
                for task in tasks:
                    kind, u, i = task
                    layer, cross, s = UNITS[u]
                    if kind in counts_side:
                        b = side_bank[counts.bank[task]]
                    if kind == "prep":
                        w = A_WIDTH[u]
                        dve.wait_ge(a_hi_ready, nth(a_hi_ready, task))
                        tt_op(A_lo[u][:, 4 * i:4 * i + 4, :].rearrange("p a b -> p (a b)"), b[:, 0:4 * w],
                              A_hi[u][:, 4 * i:4 * i + 4, :].rearrange("p a b -> p (a b)").bitcast(F32), ALU.subtract).then_inc(a_lo_ready, 1)
                    elif kind == "ln":
                        n = norm(task)
                        if i == 0:
                            dve.wait_ge(x_loaded[s], 16)
                        elif i == 3:
                            dve.wait_ge(x_ready, nth(x_ready, ("down", earlier(u), 0)))
                        else:
                            dve.wait_ge(x_ready, nth(x_ready, ("o", u if n else earlier(u), 0)))
                        for tt in range(TT):
                            last = nc.vector.bn_stats(stats[:, n, tt, :], X[s][:, tt, :])
                        last.then_inc(stats_done, 1)
                        dve.wait_ge(stats_done, nth(stats_done, task))
                        for tt in range(TT):
                            last = nc.vector.bn_aggr(mv[:, n, tt, :], stats[:, n, tt, :])
                        last.then_inc(mean_var, 1)
                        dve.wait_ge(mean_var, nth(mean_var, task))
                        nc.vector.tensor_scalar(ve[:, n, :], mv[:, n, :, 1], EPS, None, ALU.add).then_inc(var_eps, 1)
                        dve.wait_ge(rstd_ready, nth(rstd_ready, task))
                        for tt in range(TT):
                            last = nc.vector.tensor_scalar(z[:, n, tt, :], X[s][:, tt, :], mv[:, n, tt, 0:1], rstd[:, n, tt:tt + 1],
                                                           ALU.subtract, ALU.mult)
                        last.then_inc(z_ready, 1)
                        dve.wait_ge(z_ready, nth(z_ready, task))
                        if u == 0:
                            dve.wait_ge(consts_loaded, 16 * len(consts))
                        tt_op(X[s][:, :, :], X[s][:, :, :], rows[:, i, :].unsqueeze(1).to_broadcast([P, TT, D]), ALU.add)\
                            .then_inc(x_bias, 1)
                    elif kind == "split":
                        dve.wait_ge(h32_ready, nth(h32_ready, first_norm(u)))
                        if u >= 2:
                            dve.wait_ge(scores_ready, nth(scores_ready, ("scores", u - 2, LAST_SCORES)))
                        if cross:
                            nc.vector.tensor_copy(c_hi[u % 2][:, :], c32[s][:, :])
                        nc.vector.tensor_copy(h_hi[u % 2][:, :], h32[:, 0, :]).then_inc(split_hi, 1)
                        dve.wait_ge(split_hi, nth(split_hi, task))
                        if cross:
                            tt_op(c_lo[u % 2][:, :], c32[s][:, :], c_hi[u % 2][:, :].bitcast(F32), ALU.subtract)
                        tt_op(h_lo[u % 2][:, :], h32[:, 0, :], h_hi[u % 2][:, :].bitcast(F32), ALU.subtract).then_inc(split_ready, 1)
                    elif kind == "g":
                        Kd = DC if cross else D
                        dve.wait_ge(g_hi_ready, nth(g_hi_ready, task))
                        tt_op(g_lo[0:Kd, i, :], b[0:Kd, :], g_hi[0:Kd, i, :].bitcast(F32), ALU.subtract).then_inc(g_lo_ready, 1)
                    elif kind == "qk":
                        dve.wait_ge(qk_hi, nth(qk_hi, task))
                        for j in range(2):
                            c = 2 * (i % 2) + j
                            k = QK_B + (cross * 2 + i // 2) * 4 + c
                            last = nc.vector.scalar_tensor_tensor(qk_tile(u, i // 2, c), b[:, j * S:(j + 1) * S], cols[:, k:k + 1],
                                                                  qk_low[:, counts.bank[task], j, :], ALU.add, ALU.subtract)
                        last.then_inc(qk_ready, 1)
                    elif kind == "v" and layer == 1:
                        dve.wait_ge(side_ready, nth(side_ready, task))
                        tt_op(V[u % 2][:, i, 0:512], b[:, :], vrows[:, cross, :], ALU.add).then_inc(v1_ready, 1)
                    elif kind == "smax":
                        for par in range(2):
                            dve.wait_ge(smax_ready, nth(smax_ready, task, par))
                            nc.vector.tensor_reduce(mx[:, :, par, i], max_bank[par][:, :].rearrange("p (a b) -> p a b", a=TT), AX.X, ALU.max)\
                                .then_inc(max_done, 1)
                    elif kind == "mt":
                        dve.wait_ge(max_done, nth(max_done, ("smax", u, PAIRS - 1), 1))
                        nc.vector.tensor_copy(mx_hi[:, :, :, :], mx[:, :, :, :]).then_inc(max_hi, 1)
                        dve.wait_ge(max_hi, nth(max_hi, task))
                        nc.vector.tensor_copy(mx_parts[:, :, :, 0, :], mx_hi[:, :, :, :].bitcast(F32))
                        tt_op(mx_parts[:, :, :, 1, :], mx[:, :, :, :], mx_hi[:, :, :, :].bitcast(F32), ALU.subtract).then_inc(max_parts, 1)
                        dve.wait_ge(side_ready, nth(side_ready, task))
                        nc.vector.tensor_copy(MT[u % 2][0:2 * PAIRS, :], b[0:2 * PAIRS, :]).then_inc(mt_ready, 1)
                    elif kind == "rd":
                        dve.wait_ge(quad_done, nth(quad_done, ("pv", u, QUADS - 1)))
                        nc.vector.reciprocal(rd[:, :], den_bank[:, 0:S]).then_inc(den_recip, 1)
                        dve.wait_ge(den_recip, nth(den_recip, task))
                        nc.vector.tensor_copy(rd_hi[:, :], rd[:, :]).then_inc(den_hi, 1)
                        dve.wait_ge(den_hi, nth(den_hi, task))
                        tt_op(rd_lo[:, :], rd[:, :], rd_hi[:, :].bitcast(F32), ALU.subtract).then_inc(den_ready, 1)
                    elif kind == "r":
                        if i == 0:
                            dve.wait_ge(o_copied, nth(o_copied, ("pv", u, QUADS - 1)))
                        dve.wait_ge(side_ready, nth(side_ready, task))
                        o = o_un[:, o_tile(u, 2 * i):o_tile(u, 2 * i) + 2, :].rearrange("p a b -> p (a b)")
                        tt_op(o, b[:, :], o, ALU.mult).then_inc(o_scaled, 1)
                    elif kind in ("o", "down"):
                        k = layer * 3 + (cross if kind == "o" else 2)
                        dve.wait_ge(x_bias, nth(x_bias, ("ln", u, k)))
                        dve.wait_ge(side_ready, nth(side_ready, task))
                        y = b[:, 0:TT * D].rearrange("p (t d) -> p t d", t=TT)
                        if kind == "down" and layer == 1:
                            tt_op(X[s][:, :, :], y, X[s][:, :, :], ALU.add).then_inc(out_ready, 1)
                        else:
                            tt_op(X[s][:, :, :], y, X[s][:, :, :], ALU.add).then_inc(x_ready, 1)
                    elif kind == "up" and layer == 0:
                        dve.wait_ge(gelu, nth(gelu, task))
                        k = FF_B1 + i
                        nc.vector.scalar_tensor_tensor(hidden[:, i, :], b[:, 0:S], cols[:, k:k + 1], gate[:, counts.bank[task], :],
                                                       ALU.add, ALU.mult).then_inc(act0_ready, 1)


counts_side = ("prep", "ctx", "ln", "g", "qk", "v", "mt", "r", "o", "up", "down")


def arrange(i):
    f = lambda name: np.asarray(i[name])
    heads_rows = lambda w, n: np.ascontiguousarray(w.T.reshape(HEADS, 64, n).transpose(1, 0, 2))
    a = {"x": f("x"), "ctx_768": f("ctx_768")}
    for k, n in (("sa", D), ("ca", DC)):
        a[f"wqT_{k}"] = heads_rows(f(f"L0_xattn_{k}_wq"), D)
        a[f"wkT_{k}"] = heads_rows(f(f"L0_xattn_{k}_wk"), n)
    a["wv0_sa"], a["wv0_ca"] = f("L0_xattn_sa_wv"), f("L0_xattn_ca_wv")
    a["wo0"] = np.stack([f(f"L0_xattn_{k}_wo").reshape(8, P, D) for k in ("sa", "ca")]).transpose(2, 0, 1, 3)
    a["w1_0"] = f("L0_xattn_ff_w1")
    a["w2_0"] = f("L0_xattn_ff_w2").reshape(4, P, D).transpose(1, 0, 2)
    order = [4 * r + c for c in range(4) for r in range(4)]
    slots = lambda w: np.repeat(w.reshape(HEADS, 1, 8, -1)[order], 4, axis=1).reshape(512, -1)
    pad = lambda w: np.concatenate([w.reshape(HEADS, 8, -1), np.zeros((HEADS, SLOT - 8, w.shape[-1] if w.ndim > 1 else 1), w.dtype)], 1).reshape(512, -1)
    q, k = [f(f"L1_xattn_sa_w{c}") for c in "qk"]
    a["wqk1_sa"] = np.stack([slots(q).T, slots(k).T], 1)
    a["wq1_ca"], a["wk1_ca"] = slots(f("L1_xattn_ca_wq")).T, slots(f("L1_xattn_ca_wk")).T
    a["wv1_sa"], a["wv1_ca"] = pad(f("L1_xattn_sa_wv")).T, pad(f("L1_xattn_ca_wv")).T
    a["wo1"] = np.stack([pad(f(f"L1_xattn_{c}_wo").T).reshape(4, P, D) for c in ("sa", "ca")]).transpose(2, 0, 1, 3)
    a["w1_1"] = f("L1_xattn_mlp_w1").T
    a["w2_1"] = f("L1_xattn_mlp_w2").T.reshape(4, P, D).transpose(1, 0, 2)
    cols = np.zeros((P, N_COLS), np.float32)
    for layer in range(2):
        for n in range(3):
            cols[:, LN_G + layer * 3 + n] = f(f"L{layer}_xattn_ln{n + 1}_g")
            cols[:, LN_B + layer * 3 + n] = f(f"L{layer}_xattn_ln{n + 1}_b")
    cols[:, FF_B1:FF_B1 + 8] = f("L0_xattn_ff_b1").reshape(8, P).T
    cols[:, MLP_B1:MLP_B1 + 4] = f("L1_xattn_mlp_b1").reshape(4, P).T
    low = {"q": np.array([0, 0, 1, 1]), "k": np.array([0, 1, 0, 1])}
    for ci, c in enumerate(("sa", "ca")):
        for wi, w in enumerate("qk"):
            b = slots(f(f"L1_xattn_{c}_b{w}")).reshape(4, P).T
            is_low = np.repeat(np.tile(low[w], 4), 8) == 1
            n = (ci * 2 + wi) * 4
            cols[:, QK_B + n:QK_B + n + 4] = b
            cols[is_low, QK_BM + n:QK_BM + n + 4] = b[is_low]
            cols[is_low, MASK + wi] = 1
    a["cols"] = cols
    row_names = [f"L0_xattn_{n}" for n in ("sa_bo", "ca_bo", "ff_b2")] + [f"L1_xattn_{n}" for n in ("sa_bo", "ca_bo", "mlp_b2")]
    a["rows"] = np.broadcast_to(np.stack([f(n) for n in row_names]), (P, 6, D))
    a["vrows"] = np.broadcast_to(np.stack([pad(f(f"L1_xattn_{c}_bv"))[:, 0] for c in ("sa", "ca")]), (P, 2, 512))
    a["ident"] = np.eye(P, dtype=np.float32)
    selneg = np.zeros((P, PAIRS, P), np.float32)
    for t in range(PAIRS):
        selneg[[t, PAIRS + t], t] = -1
    e = np.zeros((P, QUADS, SLOT), np.float32)
    for q in range(QUADS):
        e[:, q, q] = 1
    e[:, 0, QUADS:] = 1
    sel0, sel1 = np.zeros((P, PAIRS, P), np.float32), np.zeros((P, QUADS, P), np.float32)
    for t in range(PAIRS):
        for par in range(2):
            sel0[SLOT * (2 * (t % 2) + par) + t // 2, t, 64 * par:64 * par + 64] = 1
    for c in range(QUADS):
        for j in range(4):
            sel1[SLOT * j + c, c, SLOT * j:SLOT * (j + 1)] = 1
    a["selneg"], a["e"], a["sel0"], a["sel1"] = selneg, e, sel0, sel1
    return a


def kernel(**inputs):
    import concourse.bacc as bacc
    from concourse.bass_utils import run_bass_kernel_spmd

    arrays = {f"in_{k}": np.ascontiguousarray(v) for k, v in arrange(inputs).items()}
    nc = bacc.Bacc("TRN2", target_bir_lowering=False, num_devices=1)
    args = [nc.dram_tensor(k, v.shape, mybir.dt.from_np(v.dtype), kind="ExternalInput").ap() for k, v in arrays.items()]
    out = nc.dram_tensor("out", (BATCHES, S, D), F32, kind="ExternalOutput").ap()
    build(nc, *args, out)
    r = run_bass_kernel_spmd(nc, [arrays], core_ids=[0])
    return r.results[0]["out"]
```

```python
from contextlib import ExitStack

import numpy as np
import concourse.bass as bass
from concourse import mybir

F32 = mybir.dt.float32
F32R = mybir.dt.float32r
ACT = mybir.ActivationFunctionType
ALU = mybir.AluOpType
AX = mybir.AxisListType

P = 128
BATCHES, S, D, DC = 4, 256, 128, 96
HEADS = 16
PAIRS = HEADS // 2
QUADS = HEADS // 4
HD = (64, 8)
SLOT = 32
SPLIT_PAIRS = 2
M_ROW = 24
DF = 512
TT = S // P
EPS = 1e-5
EXP_SCALE = (64 ** -0.5, 8 ** -0.5)

UNITS = [(layer, cross, s) for layer in (0, 1) for cross in (0, 1) for s in range(BATCHES)]
LAST_SCORES = TT * PAIRS - 1

LN_G, LN_B = 0, 6
FF_B1 = 12
MLP_B1 = 20
QK_B = 24
QK_BM = 40
MASK = 56
N_COLS = 58


def attention(u):
    tasks = []
    for t in range(PAIRS):
        tasks += [("scores", u, TT * t + kb) for kb in range(TT)]
        if t == 0 and u >= 1:
            tasks.append(("pv", u - 1, QUADS - 1))
        if t >= 2 and t % 2 == 0:
            tasks.append(("pv", u, t // 2 - 1))
    return tasks


def tail(u):
    layer, cross, _ = UNITS[u]
    tasks = [("rd", u, 0)] + [("r", u, i) for i in range(4 if layer == 0 else 2)] + [("o", u, 0)]
    if cross:
        tasks += [(k, u, layer * 3 + 2) for k in ("stat", "z", "ln")] + [("up", u, i) for i in range(4 if layer == 0 else 2)] + [("down", u, 0)]
    return tasks


def head(u):
    layer, cross, _ = UNITS[u]
    smax = [("smax", u, t) for t in range(PAIRS)]
    if layer == 1:
        return [("qk", u, i) for i in (0, 2, 1, 3)] + smax + [("mt", u, 0), ("mt", u, 1)]
    tasks = [("split", u, 0), ("g", u, 0)]
    for t in range(1, PAIRS):
        tasks += [("g", u, t), smax[t - 1]]
    return tasks + [smax[-1], ("mt", u, 0)]


def first_norm(u, part="ln"):
    layer, cross, _ = UNITS[u]
    return (part, u, 3 * layer + cross)


def last_norm(task):
    _, u, i = task
    if i % 3 != 2:
        return first_norm(u - 1) if u >= 1 else None
    units = [n for n in range(u) if UNITS[n][1]]
    return ("ln", units[-1], 3 * UNITS[units[-1]][0] + 2) if units else None


def values(u):
    return [("v", u, i) for i in range(4 if UNITS[u][0] == 0 else TT)]


ORDER = [
    "hhhhhhthhnhhhhththhthhhnvhthhhvhtthtvhvh",
    "hnmmhmmhmmhmhhmmhhmmmhmhmmhmhmhmhmnhhvvhvvhh",
    "mhmmmmthhmmtttthhthmmmnhhmmhhmnmmhmhmhmmmhhvhvhvvhh",
    "hmmhmmnmthmmtttthhthmmmhmmhhmmnmhhmhmmhhmmhvhvhvvhh",
    "hmmmmvthmtmttmthhthmmmhhmmmhnhmmhmhhmhmhmmnhhvhvhvh",
    "mmhhmmnmtvhmtmttthhthmmmhhmmhmhmmhmmhhmmmnhhvhhvvhh",
    "htmmhtmmmtvhmtmttthhtmtmntmhthmmhhmmnhmmhmthhmtmhmhhtthvvhtvh",
    "mmhmmvnthmmtttmthhtmmmhmhhmmtmthhmtmhhmhthmmhmnhhtthtvhtvvh",
    "mmmtvnvmmttmttmtmtnmmthhmmhhmhthmhmhmhthtthtmhmhhmmht",
    "mhmmmvmmnthhttmttnhthmmthtmvmhmthtthmthtmhmthmmmhmmhh",
    "mmhhmmmmthhmmtmmhvhmhmthmnhmntmhvhmmhmhmmhh",
    "mhmhmmmmthhmmmtmhhmtmhmhmnvhmnmthvmhhmmhmhh",
    "mmhhmmmmmvnthhmtmmhvhmhmthmnhthmmhmmhmmhhmh",
    "mmhhmmmmthhmmvnhmmhtmmhtvhmhnmmhthmmhmmhhmh",
    "mmhhmmmmmthhmmtthmmthmmthmmtvhntvhtnhthmmhtmhmmhh",
    "mhhmmmmthmhmmtmtmhthmmmthmmvmthvthththhmmmhmth",
    "mmmmmmmtmmmttmmtmtmmmttttmmmmt",
    "ttttttttttt",
]


def strands(p):
    n = len(UNITS)
    main = attention(p) if 0 <= p < n else []
    behind, ahead, val, norms = [], [], [], []
    if p == -1:
        behind = [("prep", 1, q) for q in range(QUADS)] + [("ctx", s, 0) for s in range(BATCHES)]
        ahead = [("prep", 0, q) for q in range(QUADS)]
        ahead = [first_norm(0, "stat")] + ahead + [first_norm(0, "z"), first_norm(0)]
    if p == n:
        behind += [("pv", p - 1, QUADS - 1)]
    if p == 2 * BATCHES - 3:
        behind += [("vbias", 0, cross) for cross in range(2)]
    if p >= 1:
        behind += tail(p - 1)
    if p + 1 < n:
        ahead += head(p + 1)
        if p + 2 < n:
            ahead.append(first_norm(p + 2))
            norms = [first_norm(p + 2, "stat"), first_norm(p + 2, "z")]
        val = values(p + 1)
    return {"m": main, "t": behind, "h": ahead, "v": val, "n": norms}


def plan():
    tasks = []
    for p, order in zip(range(-1, len(UNITS) + 1), ORDER, strict=True):
        left = strands(p)
        for c in order:
            tasks.append(left[c].pop(0))
        assert not any(left.values())
    return tasks


def earlier(u):
    return max(n for n in range(u) if UNITS[n][2] == UNITS[u][2])


def signals_of(task):
    kind, u, i = task
    layer, cross, _ = UNITS[u]
    if kind == "prep":
        return [("side_ready", 0), ("a_hi_ready", 0), ("a_lo_ready", 0)]
    if kind == "vbias":
        return [("side_ready", 0), ("bias_ready", 0)]
    if kind == "ctx":
        return [("side_ready", 0), ("h32_ready", 0)]
    if kind == "ln":
        return [("side_ready", 0), ("h32_ready", 0)]
    if kind == "stat":
        return [("stats_done", 0), ("mean_var", 0), ("var_eps", 0), ("rstd_ready", 0)]
    if kind == "z":
        return [("z_ready", 0), ("x_bias", 0)]
    if kind == "split":
        return [("split_hi", 0), ("split_ready", 0)]
    return {
        "g": [("side_ready", 0), ("g_hi_ready", 0), ("g_lo_ready", 0)],
        "qk": [("side_ready", 0), ("qk_hi", 0), ("qk_ready", 0)],
        "v": [("side_ready", 0), ("v_ready", 0)],
        "smax": [("smax_ready", 0), ("smax_ready", 1), ("max_done", 0), ("max_done", 1)],
        "mt": ([("max_hi", 0), ("max_parts", 0)] if i == 0 else []) + [("side_ready", 0), ("mt_ready", 0)],
        "scores": [("scores_ready", 0), ("probs_ready", 0)] + [("presum", 0)] * (i % TT == TT - 1),
        "pv": [("quad_done", 0), ("o_copied", 0)],
        "rd": [("den_recip", 0), ("den_hi", 0), ("den_ready", 0)],
        "r": [("side_ready", 0), ("o_scaled", 0)],
        "o": [("side_ready", 0), ("x_ready", 0)],
        "up": [("side_ready", 0)] + ([("gelu", 0), ("act0_ready", 0)] if layer == 0 else [("act1_ready", 0)]),
        "down": [("side_ready", 0)] + ([("x_ready", 0)] if layer == 0 else [("out_ready", 0)]),
    }[kind]


RELEASE = {"prep": "a_lo_ready", "vbias": "bias_ready", "ctx": "h32_ready", "ln": "h32_ready", "g": "g_lo_ready", "qk": "qk_ready", "mt": "mt_ready", "r": "o_scaled", "o": "x_ready"}


def release_of(task):
    kind, u, i = task
    layer = UNITS[u][0]
    if kind == "v":
        return "v_ready"
    if kind == "up":
        return "act0_ready" if layer == 0 else "act1_ready"
    if kind == "down":
        return "x_ready" if layer == 0 else "out_ready"
    return RELEASE[kind]


class Counts:

    def __init__(self, tasks):
        self.at, self.total, self.bank, self.before = {}, {}, {}, {}
        sides = []
        for task in tasks:
            for sig, part in signals_of(task):
                self.total[sig] = self.total.get(sig, 0) + 1
                self.at[sig, task, part] = self.total[sig]
                if sig == "side_ready":
                    self.bank[task] = len(sides) % 2
                    self.before[task] = sides[-2] if len(sides) >= 2 else None
                    sides.append(task)


def build(nc, x_in, ctx_in, wqT_sa, wkT_sa, wqT_ca, wkT_ca, wv0_sa, wv0_ca, wo0, w1_0, w2_0,
          wqk1_sa, wq1_ca, wk1_ca, wv1_sa, wv1_ca, wo1, w1_1, w2_1, cols_in, rows_in, vcols_in,
          ident_in, selneg_in, e_in, sel0_in, sel1_in, out):
    tasks = plan()
    counts = Counts(tasks)
    with ExitStack() as ctx:
        def sb(name, shape, dt=F32):
            return ctx.enter_context(nc.sbuf_tensor(name, shape, dt))

        A_hi = [sb("A_hi_sa", [P, HEADS, D], F32R), sb("A_hi_ca", [P, HEADS, DC], F32R)]
        A_lo = [sb("A_lo_sa", [P, HEADS, D], F32R), sb("A_lo_ca", [P, HEADS, DC], F32R)]
        wv0 = [sb("wv0_sa_s", [P, 1024]), sb("wv0_ca_s", [DC, 1024])]
        wo0_s = sb("wo0_s", [P, 2, 8, D])
        w1_0s = sb("w1_0s", [P, 2 * DF])
        w2_0s = sb("w2_0s", [P, 4, D])
        wqk1 = [sb("wqk1_sa_s", [P, 2, 512]), sb("wq1_ca_s", [P, 512])]
        wk1_cas = sb("wk1_ca_s", [DC, 512])
        wv1 = [sb("wv1_sa_s", [P, 512]), sb("wv1_ca_s", [DC, 512])]
        wo1_s = sb("wo1_s", [P, 2, 4, D])
        w1_1s = sb("w1_1s", [P, DF])
        w2_1s = sb("w2_1s", [P, 4, D])
        cols = sb("cols", [P, N_COLS])
        rows = sb("rows", [P, 6, D])
        vcols = sb("vcols", [P, 2, 4, P])
        ident = sb("ident", [P, P])
        selneg = sb("selneg", [P, PAIRS, P], F32R)
        e_cols = sb("e_cols", [P, QUADS, SLOT])
        sel0 = sb("sel0", [P, PAIRS, P], F32R)
        sel1 = sb("sel1", [P, QUADS, P], F32R)
        half_neg = sb("half_neg", [P, TT])

        X = [sb(f"x{s}", [P, TT, D]) for s in range(BATCHES)]
        c32 = [sb(f"c32_{s}", [DC, S]) for s in range(BATCHES)]

        h_hi = [sb(f"h_hi{i}", [P, S], F32R) for i in range(2)]
        h_lo = [sb(f"h_lo{i}", [P, S], F32R) for i in range(2)]
        c_hi = [sb(f"c_hi{i}", [DC + 2, S], F32R) for i in range(2)]
        c_lo = [sb(f"c_lo{i}", [DC, S], F32R) for i in range(2)]

        stats = sb("stats", [P, 2, TT, 6])
        mv = sb("mv", [P, 2, TT, 2])
        ve = sb("ve", [P, 2, TT])
        rstd = sb("rstd", [P, 2, TT])
        z = sb("z", [P, 2, TT, D])
        h32 = sb("h32", [P, 2, S])

        g_hi = sb("g_hi", [P, PAIRS, 2 * S], F32R)
        g_lo = sb("g_lo", [P, PAIRS, 2 * S], F32R)
        qk1 = [g_hi, g_lo]
        V = [sb(f"v{i}", [P, TT, 1024]) for i in range(2)]
        probs = sb("probs", [P, 4, TT, 2 * S])
        psums = sb("psums", [P, 4, 2 * S])
        o_un = sb("o_un", [P, PAIRS, S])
        rd = sb("rd", [P, S])
        rd_hi = sb("rd_hi", [P, S], F32R)
        rd_lo = sb("rd_lo", [P, S], F32R)
        mx = sb("mx", [P, TT, 2, PAIRS])
        mx_hi = sb("mx_hi", [P, TT, 2, PAIRS], F32R)
        mx_parts = sb("mx_parts", [P, TT, 2, 2, PAIRS])
        mx_slots = wo0_s[:, 0, :, :].rearrange("p (t c) r -> p t c r", t=TT)
        MT = [sb(f"mt{i}", [P, 2 * S], F32R) for i in range(2)]
        qk_low = sb("qk_low", [P, 2, 2, S])
        gate = sb("gate", [P, 2, S])
        hidden = sb("hidden", [P, 4, S])
        C = [hidden[:, s, 0:TT * DC].rearrange("p (t d) -> p t d", t=TT) for s in range(BATCHES)]

        banks = [ctx.enter_context(nc.psum_tensor(f"bank{i}", [P, 512], F32)) for i in range(8)]
        max_bank = banks[0:2]
        score_bank = banks[2:4]
        pv_bank = banks[4]
        den_bank = banks[6]
        side_bank = [banks[5], banks[7]]

        sem = lambda name: ctx.enter_context(nc.semaphore(name))
        side_ready, smax_ready, scores_ready, quad_done = sem("side_ready"), sem("smax_ready"), sem("scores_ready"), sem("quad_done")
        stats_done, mean_var, var_eps, rstd_ready = sem("stats_done"), sem("mean_var"), sem("var_eps"), sem("rstd_ready")
        z_ready, h32_ready, split_hi, split_ready = sem("z_ready"), sem("h32_ready"), sem("split_hi"), sem("split_ready")
        a_hi_ready, a_lo_ready = sem("a_hi_ready"), sem("a_lo_ready")
        g_hi_ready, g_lo_ready, qk_hi, qk_ready = sem("g_hi_ready"), sem("g_lo_ready"), sem("qk_hi"), sem("qk_ready")
        v_ready, bias_ready = sem("v_ready"), sem("bias_ready")
        max_done, max_hi, max_parts, mt_ready = sem("max_done"), sem("max_hi"), sem("max_parts"), sem("mt_ready")
        probs_ready, presum, o_copied = sem("probs_ready"), sem("presum"), sem("o_copied")
        den_recip, den_hi, den_ready, o_scaled = sem("den_recip"), sem("den_hi"), sem("den_ready"), sem("o_scaled")
        x_bias, x_ready, out_ready = sem("x_bias"), sem("x_ready"), sem("out_ready")
        gelu, act0_ready, act1_ready = sem("gelu"), sem("act0_ready"), sem("act1_ready")
        sems = {x.name: x for x in (
            side_ready, smax_ready, scores_ready, quad_done, stats_done, mean_var, var_eps, rstd_ready, z_ready, h32_ready,
            split_hi, split_ready, g_hi_ready, g_lo_ready, qk_hi, qk_ready, v_ready, bias_ready, max_done, max_hi, max_parts,
            mt_ready, probs_ready, presum, o_copied, den_recip, den_hi, den_ready, o_scaled, x_bias, x_ready, out_ready,
            gelu, act0_ready, act1_ready, a_hi_ready, a_lo_ready)}
        assert set(counts.total) == set(sems)
        x_loaded = [sem(f"x{s}_loaded") for s in range(BATCHES)]
        c_loaded = sem("contexts_loaded")
        stored = sem("stored")
        w_a = [sem("wqk_sa_loaded"), sem("wqk_ca_loaded")]
        consts_loaded, selectors_loaded = sem("consts_loaded"), sem("selectors_loaded")
        consts_set = sem("consts_set")
        max_placed = sem("max_placed")

        consts = [(ident, ident_in), (cols, cols_in), (e_cols, e_in), (rows, rows_in)]
        weights = {
            "wv0": [(wv0[0], wv0_sa), (wv0[1], wv0_ca)],
            "rest0": [(wo0_s, wo0), (w1_0s, w1_0), (w2_0s, w2_0)],
            "qkv1": [(wqk1[0], wqk1_sa), (wqk1[1], wq1_ca), (wk1_cas, wk1_ca), (wv1[0], wv1_sa), (wv1[1], wv1_ca)],
            "rest1": [(w1_1s, w1_1), (w2_1s, w2_1)],
            "out1": [(wo1_s, wo1), (vcols, vcols_in)],
        }
        w_loaded = {k: sem(f"{k}_loaded") for k in weights}
        casts = [(selneg, selneg_in), (sel0, sel0_in), (sel1, sel1_in)]

        def full(t):
            return t[tuple(slice(None) for _ in t.shape)]

        stage_q = [probs[0:64, 0:2, :, :].rearrange("p a b c -> p (a b c)").rearrange("p (h d) -> p h d", h=HEADS),
                   o_un[0:64, :, :].rearrange("p a b -> p (a b)").rearrange("p (h d) -> p h d", h=HEADS)]
        stage_k = [probs[0:64, 2:4, :, :].rearrange("p a b c -> p (a b c)").rearrange("p (h d) -> p h d", h=HEADS),
                   V[1][0:64, :, :].rearrange("p a b -> p (a b)")[:, 0:HEADS * DC].rearrange("p (h d) -> p h d", h=HEADS)]
        A_WIDTH = (D, DC)

        def nth(signal, task, part=0):
            return counts.at[signal.name, task, part]

        def qk_tile(u, which, c):
            t = qk1[u % 2]
            return t[:, 2 * which + c // 2, (c % 2) * S:(c % 2 + 1) * S]

        def o_tile(u, k):
            return k + (4 * (u % 2) if UNITS[u][0] == 1 else 0)

        def norm(task):
            return int(task[2] % 3 == 2)

        with nc.Block() as block:
            @block.sync
            def _(sp):
                sp.dma_start(stage_q[0], wqT_sa).then_inc(w_a[0], 16)
                sp.dma_start(X[0][:, :, :], x_in[0].rearrange("(t p) d -> p t d", p=P)).then_inc(x_loaded[0], 16)
                for dst, src in consts:
                    sp.dma_start(full(dst), src).then_inc(consts_loaded, 16)
                sp.dma_start(stage_q[1], wqT_ca).then_inc(w_a[1], 16)
                for dst, src in weights["wv0"]:
                    sp.dma_start(full(dst), src).then_inc(w_loaded["wv0"], 16)
                for s in range(1, BATCHES):
                    sp.dma_start(X[s][:, :, :], x_in[s].rearrange("(t p) d -> p t d", p=P)).then_inc(x_loaded[s], 16)
                for s in range(BATCHES):
                    sp.dma_start(C[s], ctx_in[s].rearrange("(t p) d -> p t d", p=P)).then_inc(c_loaded, 16)
                for k in ("rest0", "out1", "qkv1", "rest1"):
                    for dst, src in weights[k]:
                        sp.dma_start(full(dst), src).then_inc(w_loaded[k], 16)
                for s in range(BATCHES):
                    task = ("down", len(UNITS) - BATCHES + s, 0)
                    sp.wait_ge(out_ready, nth(out_ready, task))
                    sp.dma_start(out[s].rearrange("(t p) d -> p t d", p=P), X[s][:, :, :]).then_inc(stored, 16)
                sp.wait_ge(stored, 16 * BATCHES)

            @block.gpsimd
            def _(pool):
                nc.gpsimd.memset(half_neg[:, :], -0.5).then_inc(consts_set, 1)
                for i in range(2):
                    nc.gpsimd.memset(MT[i][:, :].bitcast(F32), 0.0).then_inc(consts_set, 1)
                for dst, src in casts:
                    pool.dma_start(full(dst), src).then_inc(selectors_loaded, 16)
                pool.wait_ge(consts_set, 5)
                for task in tasks:
                    kind, u, i = task
                    layer, cross, s = UNITS[u]
                    if kind == "stat" and task == first_norm(2 * BATCHES - 2, "stat"):
                        pool.wait_ge(x_ready, nth(x_ready, ("o", BATCHES - 1, 0)))
                        nc.gpsimd.memset(mx_slots[:, :, :, :], 0.0).then_inc(consts_set, 1)
                    if kind == "stat":
                        n = norm(task)
                        pool.wait_ge(var_eps, nth(var_eps, task))
                        nc.gpsimd.tensor_tensor(rstd[:, n, :], ve[:, n, :], half_neg[:, :], ALU.pow).then_inc(rstd_ready, 1)
                    if kind == "z":
                        pool.wait_ge(z_ready, nth(z_ready, task))
                        if u == 0:
                            pool.wait_ge(consts_loaded, 16 * len(consts))
                        if i in (3, 4) and u in (2 * BATCHES, 3 * BATCHES):
                            pool.wait_ge(bias_ready, nth(bias_ready, ("vbias", 0, i - 3)))
                        nc.gpsimd.tensor_tensor(X[s][:, :, :], X[s][:, :, :], rows[:, i, :].unsqueeze(1).to_broadcast([P, TT, D]), ALU.add)\
                            .then_inc(x_bias, 1)
                    if kind == "scores" and i == 0 and (layer, cross) == (0, 1):
                        pool.wait_ge(mt_ready, nth(mt_ready, ("mt", u, 0)))
                        pool.wait_ge(scores_ready, nth(scores_ready, ("scores", u - 1, LAST_SCORES)))
                        for e in range(2):
                            pool.dma_start(g_hi[DC + e:DC + e + 1, SPLIT_PAIRS:PAIRS, :],
                                           MT[u % 2][e * PAIRS + SPLIT_PAIRS:(e + 1) * PAIRS, :]).then_inc(max_placed, 16)
                    if kind == "scores" and i % TT == TT - 1:
                        t = i // TT
                        pool.wait_ge(probs_ready, nth(probs_ready, task))
                        if t >= 4:
                            pool.wait_ge(quad_done, nth(quad_done, ("pv", u, t // 2 - 2)))
                        elif u >= 1:
                            pool.wait_ge(quad_done, nth(quad_done, ("pv", u - 1, QUADS - 2 + t // 2)))
                        nc.gpsimd.tensor_tensor(psums[:, t % 4, :], probs[:, t % 4, 0, :], probs[:, t % 4, 1, :], ALU.add)\
                            .then_inc(presum, 1)

            @block.tensor
            def _(pe):
                mm = nc.tensor.matmul
                def side(task):
                    before = counts.before[task]
                    if before is not None:
                        freed = sems[release_of(before)]
                        pe.wait_ge(freed, nth(freed, before))
                    return side_bank[counts.bank[task]]

                for n, task in enumerate(tasks):
                    kind, u, i = task
                    layer, cross, s = UNITS[u]
                    Kd = DC if cross else D
                    if kind == "prep":
                        b = side(task)
                        w = A_WIDTH[u]
                        if i == 0:
                            pe.wait_ge(w_a[u], 32)
                        for j in range(4):
                            last = mm(b[:, j * w:(j + 1) * w], stage_q[u][:, 4 * i + j, :], stage_k[u][:, 4 * i + j, :],
                                      start=True, stop=True)
                        last.then_inc(side_ready, 1)
                    elif kind == "vbias":
                        b = side(task)
                        if i == 0:
                            pe.wait_ge(w_loaded["out1"], 16 * len(weights["out1"]))
                        for k in range(4):
                            last = mm(b[:, 0:D], vcols[:, i, k, :], wo1_s[:, i, k, :], start=(k == 0), stop=(k == 3))
                        last.then_inc(side_ready, 1)
                    elif kind == "ctx":
                        b = side(task)
                        if u == 0:
                            pe.wait_ge(c_loaded, 16 * BATCHES)
                            pe.wait_ge(consts_loaded, 16 * len(consts))
                        for tt in range(TT):
                            last = nc.tensor.transpose(b[0:DC, tt * P:(tt + 1) * P], C[u][:, tt, :], ident[:, :])
                        last.then_inc(side_ready, 1)
                    elif kind == "ln":
                        b = side(task)
                        pe.wait_ge(z_ready, nth(z_ready, ("z", u, i)))
                        if u == 0:
                            pe.wait_ge(consts_loaded, 16 * len(consts))
                        for tt in range(TT):
                            last = nc.tensor.transpose(b[:, tt * P:(tt + 1) * P], z[:, norm(task), tt, :], ident[:, :])
                        last.then_inc(side_ready, 1)
                    elif kind == "g":
                        b = side(task)
                        if i == 0:
                            pe.wait_ge(split_ready, nth(split_ready, ("split", u, 0)))
                        if u in (0, BATCHES) and i % 2 == 0:
                            pe.wait_ge(a_lo_ready, nth(a_lo_ready, ("prep", cross, i // 2)))
                        for j in range(2):
                            h = 2 * i + j
                            o = b[0:Kd, j * S:(j + 1) * S]
                            mm(o, A_hi[cross][:, h, :], h_hi[u % 2][:, :], start=True, stop=False)
                            mm(o, A_hi[cross][:, h, :], h_lo[u % 2][:, :], start=False, stop=False)
                            last = mm(o, A_lo[cross][:, h, :], h_hi[u % 2][:, :], start=False, stop=True)
                        last.then_inc(side_ready, 1)
                    elif kind == "qk":
                        b = side(task)
                        if i == 0:
                            pe.wait_ge(h32_ready, nth(h32_ready, ("ln", u, 3 + cross)))
                            if u == 2 * BATCHES:
                                pe.wait_ge(w_loaded["qkv1"], 16 * len(weights["qkv1"]))
                        for j in range(2):
                            c = 2 * (i % 2) + j
                            if i // 2 == 0:
                                w, act = (wqk1[1] if cross else wqk1[0][:, 0, :]), h32[:, 0, :]
                            elif cross:
                                w, act = wk1_cas, c32[s][:, :]
                            else:
                                w, act = wqk1[0][:, 1, :], h32[:, 0, :]
                            last = mm(b[:, j * S:(j + 1) * S], w[:, c * P:(c + 1) * P], act, start=True, stop=True)
                        last.then_inc(side_ready, 1)
                    elif kind == "v":
                        b = side(task)
                        if i == 0:
                            pe.wait_ge(h32_ready, nth(h32_ready, ("ctx", s, 0) if cross else ("ln", u, layer * 3)))
                        if u == 0 and i == 0:
                            pe.wait_ge(w_loaded["wv0"], 16 * len(weights["wv0"]))
                        if u == 2 * BATCHES and i == 0:
                            pe.wait_ge(w_loaded["qkv1"], 16 * len(weights["qkv1"]))
                        tt, half = (i % 2, i // 2) if layer == 0 else (i, 0)
                        w = wv0[cross] if layer == 0 else wv1[cross]
                        act = c32[s] if cross else h32[:, 0, :]
                        last = mm(b[:, :], act[:, tt * P:(tt + 1) * P], w[:, half * 512:(half + 1) * 512], start=True, stop=True)
                        last.then_inc(side_ready, 1)
                    elif kind == "smax":
                        for par in range(2):
                            h = 2 * i + par
                            if i >= 1:
                                pe.wait_ge(max_done, nth(max_done, ("smax", u, i - 1), par))
                            elif u >= 1:
                                pe.wait_ge(max_done, nth(max_done, ("smax", u - 1, PAIRS - 1), par))
                            if par == 0:
                                if layer == 0:
                                    pe.wait_ge(g_lo_ready, nth(g_lo_ready, ("g", u, i)))
                                elif i == 0:
                                    pe.wait_ge(qk_ready, nth(qk_ready, ("qk", u, 3)))
                            for qt in range(TT):
                                o = max_bank[par][:, qt * S:(qt + 1) * S]
                                if layer == 0:
                                    q0 = par * S + qt * P
                                    last = mm(o, g_hi[0:Kd, i, q0:q0 + P], (c_hi if cross else h_hi)[u % 2][0:Kd, :], start=True, stop=True)
                                else:
                                    c, r = h % 4, SLOT * (h // 4)
                                    last = mm(o, qk_tile(u, 0, c)[r:r + SLOT, qt * P:(qt + 1) * P],
                                              qk_tile(u, 1, c)[r:r + SLOT, :], start=True, stop=True, tile_position=(r, 0))
                            last.then_inc(smax_ready, 1)
                    elif kind == "mt":
                        b = side(task)
                        if i == 0:
                            pe.wait_ge(max_parts, nth(max_parts, task))
                        for par in range(2):
                            for qt in range(TT):
                                cs = slice(par * S + qt * P, par * S + (qt + 1) * P)
                                if layer == 0:
                                    last = nc.tensor.transpose(b[0:2 * PAIRS, cs], mx_parts[:, qt, par, :, :].rearrange("p a b -> p (a b)"), ident[:, :])
                                else:
                                    last = nc.tensor.transpose(b[:, cs], mx_slots[:, qt, 2 * i + par, :], ident[:, :])
                        last.then_inc(side_ready, 1)
                    elif kind == "scores":
                        t, kb = divmod(i, TT)
                        if i == 0:
                            pe.wait_ge(mt_ready, nth(mt_ready, ("mt", u, 0)))
                        if layer == 1 and t == 1 and kb == 0:
                            pe.wait_ge(mt_ready, nth(mt_ready, ("mt", u, 1)))
                        if i == 0 and u == 0:
                            pe.wait_ge(selectors_loaded, 16 * len(casts))
                            pe.wait_ge(consts_set, 5)
                        if t >= 1:
                            pe.wait_ge(probs_ready, nth(probs_ready, ("scores", u, i - TT)))
                        elif u >= 1:
                            pe.wait_ge(probs_ready, nth(probs_ready, ("scores", u - 1, TT * (PAIRS - 1) + kb)))
                        o = score_bank[kb]
                        ks = slice(kb * P, (kb + 1) * P)
                        if layer == 0:
                            below = cross == 1 and t >= SPLIT_PAIRS
                            if below and i == TT * SPLIT_PAIRS:
                                pe.wait_ge(max_placed, 32 * (u - BATCHES + 1))
                            if not below:
                                mm(o[:, :], selneg[:, t, :], MT[u % 2][:, :], start=True, stop=False)
                            k_hi, k_lo = (c_hi, c_lo) if cross else (h_hi, h_lo)
                            K1 = Kd + 2 * below
                            mm(o[:, :], k_hi[u % 2][0:K1, ks], g_hi[0:K1, t, :], start=below, stop=False)
                            mm(o[:, :], k_hi[u % 2][0:Kd, ks], g_lo[0:Kd, t, :], start=False, stop=False)
                            last = mm(o[:, :], k_lo[u % 2][:, ks], g_hi[0:Kd, t, :], start=False, stop=True)
                        else:
                            for par in range(2):
                                h = 2 * t + par
                                c, r = h % 4, SLOT * (h // 4)
                                last = mm(o[:, par * S:(par + 1) * S], qk_tile(u, 1, c)[r:r + SLOT, ks],
                                          qk_tile(u, 0, c)[r:r + SLOT, :], start=True, stop=True, tile_position=(r, 0))
                        last.then_inc(scores_ready, 1)
                    elif kind == "pv":
                        pe.wait_ge(probs_ready, nth(probs_ready, ("scores", u, 2 * TT * (i + 1) - 1)))
                        if i >= 1:
                            pe.wait_ge(o_copied, nth(o_copied, ("pv", u, i - 1)))
                        elif u >= 1:
                            pe.wait_ge(o_copied, nth(o_copied, ("pv", u - 1, QUADS - 1)))
                        if i == 0:
                            for k in range(4 if layer == 0 else TT):
                                pe.wait_ge(v_ready, nth(v_ready, ("v", u, k)))
                        if layer == 0:
                            for t in (2 * i, 2 * i + 1):
                                for kb in range(TT):
                                    for par in range(2):
                                        h = 2 * t + par
                                        mm(pv_bank[64 * par:64 * par + 64, (t % 2) * S:(t % 2 + 1) * S],
                                           V[u % 2][:, kb, h * 64:(h + 1) * 64], probs[:, t % 4, kb, par * S:(par + 1) * S],
                                           start=(kb == 0), stop=(kb == TT - 1))
                        else:
                            for kb in range(TT):
                                for j in range(4):
                                    h = 4 * i + j
                                    mm(pv_bank[SLOT * j:SLOT * (j + 1), 0:S], V[u % 2][:, kb, h * SLOT:(h + 1) * SLOT],
                                       probs[:, (h // 2) % 4, kb, (h % 2) * S:(h % 2 + 1) * S],
                                       start=(kb == 0), stop=(kb == TT - 1), tile_position=(0, SLOT * j))
                        pe.wait_ge(presum, nth(presum, ("scores", u, 2 * TT * (i + 1) - 1)))
                        if i == 0 and u >= 1:
                            pe.wait_ge(den_recip, nth(den_recip, ("rd", u - 1, 0)))
                        for j in range(4):
                            last = mm(den_bank[SLOT * j:SLOT * (j + 1), 0:S], e_cols[:, i, :],
                                      psums[:, (2 * i + j // 2) % 4, (j % 2) * S:(j % 2 + 1) * S],
                                      start=(i == 0), stop=(i == QUADS - 1), tile_position=(0, SLOT * j))
                        last.then_inc(quad_done, 1)
                    elif kind == "r":
                        b = side(task)
                        if i == 0:
                            pe.wait_ge(den_ready, nth(den_ready, ("rd", u, 0)))
                        for j in range(2):
                            w = (sel0 if layer == 0 else sel1)[:, 2 * i + j, :]
                            mm(b[:, j * S:(j + 1) * S], w, rd_hi[:, :], start=True, stop=False)
                            last = mm(b[:, j * S:(j + 1) * S], w, rd_lo[:, :], start=False, stop=True)
                        last.then_inc(side_ready, 1)
                    elif kind == "o":
                        b = side(task)
                        tiles = 8 if layer == 0 else 4
                        pe.wait_ge(o_scaled, nth(o_scaled, ("r", u, tiles // 2 - 1)))
                        w = wo0_s if layer == 0 else wo1_s
                        if u in (0, 2 * BATCHES):
                            group = "rest0" if layer == 0 else "out1"
                            pe.wait_ge(w_loaded[group], 16 * len(weights[group]))
                        for tt in range(TT):
                            for k in range(tiles):
                                last = mm(b[:, tt * D:(tt + 1) * D], o_un[:, o_tile(u, k), tt * P:(tt + 1) * P], w[:, cross, k, :],
                                          start=(k == 0), stop=(k == tiles - 1))
                        last.then_inc(side_ready, 1)
                    elif kind == "up":
                        b = side(task)
                        if i == 0:
                            pe.wait_ge(h32_ready, nth(h32_ready, ("ln", u, layer * 3 + 2)))
                            if u == 3 * BATCHES:
                                pe.wait_ge(w_loaded["rest1"], 16 * len(weights["rest1"]))
                        for j in range(2):
                            c = (i + 4 * j) if layer == 0 else (2 * i + j)
                            w = w1_0s if layer == 0 else w1_1s
                            last = mm(b[:, j * S:(j + 1) * S], w[:, c * P:(c + 1) * P], h32[:, 1, :], start=True, stop=True)
                        last.then_inc(side_ready, 1)
                    elif kind == "down":
                        b = side(task)
                        if layer == 0:
                            pe.wait_ge(act0_ready, nth(act0_ready, ("up", u, 3)))
                        else:
                            pe.wait_ge(act1_ready, nth(act1_ready, ("up", u, 1)))
                        w = w2_0s if layer == 0 else w2_1s
                        for tt in range(TT):
                            for k in range(4):
                                last = mm(b[:, tt * D:(tt + 1) * D], hidden[:, k, tt * P:(tt + 1) * P], w[:, k, :],
                                          start=(k == 0), stop=(k == 3))
                        last.then_inc(side_ready, 1)

            @block.scalar
            def _(act):
                act.dma_start(stage_k[0], wkT_sa).then_inc(w_a[0], 16)
                act.dma_start(stage_k[1], wkT_ca).then_inc(w_a[1], 16)
                for task in tasks:
                    kind, u, i = task
                    layer, cross, s = UNITS[u]
                    if kind in counts_side:
                        b = side_bank[counts.bank[task]]
                    if kind == "prep":
                        w = A_WIDTH[u]
                        act.wait_ge(side_ready, nth(side_ready, task))
                        nc.scalar.activation(A_hi[u][:, 4 * i:4 * i + 4, :].rearrange("p a b -> p (a b)"), b[:, 0:4 * w], ACT.Copy)\
                            .then_inc(a_hi_ready, 1)
                    elif kind == "ctx":
                        act.wait_ge(side_ready, nth(side_ready, task))
                        nc.scalar.activation(c32[u][:, :], b[0:DC, 0:S], ACT.Copy).then_inc(h32_ready, 1)
                    elif kind == "ln":
                        if u == 0:
                            act.wait_ge(consts_loaded, 16 * len(consts))
                        act.wait_ge(side_ready, nth(side_ready, task))
                        nc.scalar.activation(h32[:, norm(task), :], b[:, 0:S], ACT.Identity, scale=cols[:, LN_G + i:LN_G + i + 1],
                                             bias=cols[:, LN_B + i:LN_B + i + 1]).then_inc(h32_ready, 1)
                    elif kind == "g":
                        Kd = DC if cross else D
                        act.wait_ge(side_ready, nth(side_ready, task))
                        nc.scalar.activation(g_hi[0:Kd, i, :], b[0:Kd, :], ACT.Copy).then_inc(g_hi_ready, 1)
                    elif kind == "qk":
                        act.wait_ge(side_ready, nth(side_ready, task))
                        for j in range(2):
                            k = QK_BM + (cross * 2 + i // 2) * 4 + 2 * (i % 2) + j
                            m = MASK + i // 2
                            last = nc.scalar.activation(qk_low[:, counts.bank[task], j, :].bitcast(F32R), b[:, j * S:(j + 1) * S], ACT.Identity,
                                                        scale=cols[:, m:m + 1], bias=cols[:, k:k + 1])
                        last.then_inc(qk_hi, 1)
                    elif kind == "v":
                        act.wait_ge(side_ready, nth(side_ready, task))
                        tt, half = i % 2, i // 2
                        nc.scalar.activation(V[u % 2][:, tt, half * 512:(half + 1) * 512], b[:, :], ACT.Copy).then_inc(v_ready, 1)
                    elif kind == "scores":
                        t, kb = divmod(i, TT)
                        act.wait_ge(scores_ready, nth(scores_ready, task))
                        nc.scalar.activation(probs[:, t % 4, kb, :], score_bank[kb][:, :], ACT.Exp, scale=EXP_SCALE[layer])\
                            .then_inc(probs_ready, 1)
                    elif kind == "rd":
                        act.wait_ge(den_recip, nth(den_recip, task))
                        nc.scalar.activation(rd_hi[:, :], rd[:, :], ACT.Copy).then_inc(den_hi, 1)
                    elif kind == "pv":
                        act.wait_ge(quad_done, nth(quad_done, task))
                        if layer == 0:
                            dst = o_un[:, 2 * i:2 * i + 2, :].rearrange("p a b -> p (a b)")
                            nc.scalar.activation(dst, pv_bank[:, :], ACT.Copy).then_inc(o_copied, 1)
                        else:
                            nc.scalar.activation(o_un[:, o_tile(u, i), :], pv_bank[:, 0:S], ACT.Copy).then_inc(o_copied, 1)
                    elif kind == "up":
                        act.wait_ge(side_ready, nth(side_ready, task))
                        if layer == 0:
                            k = FF_B1 + 4 + i
                            nc.scalar.activation(gate[:, counts.bank[task], :], b[:, S:2 * S], ACT.Gelu, bias=cols[:, k:k + 1])\
                                .then_inc(gelu, 1)
                        else:
                            for j in range(2):
                                k = MLP_B1 + 2 * i + j
                                last = nc.scalar.activation(hidden[:, 2 * i + j, :], b[:, j * S:(j + 1) * S], ACT.Gelu, bias=cols[:, k:k + 1])
                            last.then_inc(act1_ready, 1)

            @block.vector
            def _(dve):
                tt_op = nc.vector.tensor_tensor
                for i in range(2):
                    nc.vector.memset(c_hi[i][DC:DC + 2, :].bitcast(F32), -1.0).then_inc(consts_set, 1)
                for task in tasks:
                    kind, u, i = task
                    layer, cross, s = UNITS[u]
                    if kind in counts_side:
                        b = side_bank[counts.bank[task]]
                    if kind == "prep":
                        w = A_WIDTH[u]
                        dve.wait_ge(a_hi_ready, nth(a_hi_ready, task))
                        tt_op(A_lo[u][:, 4 * i:4 * i + 4, :].rearrange("p a b -> p (a b)"), b[:, 0:4 * w],
                              A_hi[u][:, 4 * i:4 * i + 4, :].rearrange("p a b -> p (a b)").bitcast(F32), ALU.subtract).then_inc(a_lo_ready, 1)
                    elif kind == "stat":
                        n = norm(task)
                        if i == 0:
                            dve.wait_ge(x_loaded[s], 16)
                        elif i == 3:
                            dve.wait_ge(x_ready, nth(x_ready, ("down", earlier(u), 0)))
                        else:
                            dve.wait_ge(x_ready, nth(x_ready, ("o", u if n else earlier(u), 0)))
                        for tt in range(TT):
                            last = nc.vector.bn_stats(stats[:, n, tt, :], X[s][:, tt, :])
                        last.then_inc(stats_done, 1)
                        dve.wait_ge(stats_done, nth(stats_done, task))
                        for tt in range(TT):
                            last = nc.vector.bn_aggr(mv[:, n, tt, :], stats[:, n, tt, :])
                        last.then_inc(mean_var, 1)
                        dve.wait_ge(mean_var, nth(mean_var, task))
                        nc.vector.tensor_scalar(ve[:, n, :], mv[:, n, :, 1], EPS, None, ALU.add).then_inc(var_eps, 1)
                    elif kind == "z":
                        n = norm(task)
                        dve.wait_ge(rstd_ready, nth(rstd_ready, ("stat", u, i)))
                        if last_norm(task):
                            dve.wait_ge(h32_ready, nth(h32_ready, last_norm(task)))
                        for tt in range(TT):
                            last = nc.vector.tensor_scalar(z[:, n, tt, :], X[s][:, tt, :], mv[:, n, tt, 0:1], rstd[:, n, tt:tt + 1],
                                                           ALU.subtract, ALU.mult)
                        last.then_inc(z_ready, 1)
                    elif kind == "split":
                        dve.wait_ge(h32_ready, nth(h32_ready, first_norm(u)))
                        if u >= 2:
                            dve.wait_ge(scores_ready, nth(scores_ready, ("scores", u - 2, LAST_SCORES)))
                        if cross:
                            nc.vector.tensor_copy(c_hi[u % 2][0:DC, :], c32[s][:, :])
                        nc.vector.tensor_copy(h_hi[u % 2][:, :], h32[:, 0, :]).then_inc(split_hi, 1)
                        dve.wait_ge(split_hi, nth(split_hi, task))
                        if cross:
                            tt_op(c_lo[u % 2][:, :], c32[s][:, :], c_hi[u % 2][0:DC, :].bitcast(F32), ALU.subtract)
                        tt_op(h_lo[u % 2][:, :], h32[:, 0, :], h_hi[u % 2][:, :].bitcast(F32), ALU.subtract).then_inc(split_ready, 1)
                    elif kind == "g":
                        Kd = DC if cross else D
                        dve.wait_ge(g_hi_ready, nth(g_hi_ready, task))
                        tt_op(g_lo[0:Kd, i, :], b[0:Kd, :], g_hi[0:Kd, i, :].bitcast(F32), ALU.subtract).then_inc(g_lo_ready, 1)
                    elif kind == "qk":
                        dve.wait_ge(qk_hi, nth(qk_hi, task))
                        for j in range(2):
                            c = 2 * (i % 2) + j
                            k = QK_B + (cross * 2 + i // 2) * 4 + c
                            last = nc.vector.scalar_tensor_tensor(qk_tile(u, i // 2, c), b[:, j * S:(j + 1) * S], cols[:, k:k + 1],
                                                                  qk_low[:, counts.bank[task], j, :], ALU.add, ALU.subtract)
                        last.then_inc(qk_ready, 1)
                    elif kind == "vbias":
                        dve.wait_ge(side_ready, nth(side_ready, task))
                        tt_op(rows[:, 3 + i, :], b[:, 0:D], rows[:, 3 + i, :], ALU.add).then_inc(bias_ready, 1)
                    elif kind == "smax":
                        for par in range(2):
                            dve.wait_ge(smax_ready, nth(smax_ready, task, par))
                            nc.vector.tensor_reduce(mx[:, :, par, i], max_bank[par][:, :].rearrange("p (a b) -> p a b", a=TT), AX.X, ALU.max)\
                                .then_inc(max_done, 1)
                    elif kind == "mt":
                        if i == 0:
                            dve.wait_ge(max_done, nth(max_done, ("smax", u, PAIRS - 1), 1))
                            nc.vector.tensor_copy(mx_hi[:, :, :, :], mx[:, :, :, :]).then_inc(max_hi, 1)
                            dve.wait_ge(max_hi, nth(max_hi, task))
                            if layer == 0:
                                nc.vector.tensor_copy(mx_parts[:, :, :, 0, :], mx_hi[:, :, :, :].bitcast(F32))
                                tt_op(mx_parts[:, :, :, 1, :], mx[:, :, :, :], mx_hi[:, :, :, :].bitcast(F32), ALU.subtract).then_inc(max_parts, 1)
                            else:
                                if u == 2 * BATCHES:
                                    dve.wait_ge(consts_set, 6)
                                for qt in range(TT):
                                    high, low = (mx_slots[:, qt, :, :].rearrange("p (c par) (a r) -> p par c a r", par=2, r=SLOT)[:, :, :, :, M_ROW + e]
                                                 for e in range(2))
                                    by_head = lambda x: x[:, qt, :, :].rearrange("p par (a c) -> p par c a", c=2)
                                    nc.vector.tensor_copy(high, by_head(mx_hi).bitcast(F32))
                                    last = tt_op(low, by_head(mx), by_head(mx_hi).bitcast(F32), ALU.subtract)
                                last.then_inc(max_parts, 1)
                        dve.wait_ge(side_ready, nth(side_ready, task))
                        if layer == 0:
                            nc.vector.tensor_copy(MT[u % 2][0:2 * PAIRS, :], b[0:2 * PAIRS, :]).then_inc(mt_ready, 1)
                        else:
                            q2 = qk1[u % 2][:, i, :]
                            tt_op(q2, b[:, :], q2.bitcast(F32), ALU.add).then_inc(mt_ready, 1)
                    elif kind == "rd":
                        dve.wait_ge(quad_done, nth(quad_done, ("pv", u, QUADS - 1)))
                        nc.vector.reciprocal(rd[:, :], den_bank[:, 0:S]).then_inc(den_recip, 1)
                        dve.wait_ge(den_hi, nth(den_hi, task))
                        tt_op(rd_lo[:, :], rd[:, :], rd_hi[:, :].bitcast(F32), ALU.subtract).then_inc(den_ready, 1)
                    elif kind == "r":
                        if i == 0:
                            dve.wait_ge(o_copied, nth(o_copied, ("pv", u, QUADS - 1)))
                        dve.wait_ge(side_ready, nth(side_ready, task))
                        o = o_un[:, o_tile(u, 2 * i):o_tile(u, 2 * i) + 2, :].rearrange("p a b -> p (a b)")
                        tt_op(o, b[:, :], o, ALU.mult).then_inc(o_scaled, 1)
                    elif kind in ("o", "down"):
                        k = layer * 3 + (cross if kind == "o" else 2)
                        dve.wait_ge(x_bias, nth(x_bias, ("z", u, k)))
                        dve.wait_ge(side_ready, nth(side_ready, task))
                        y = b[:, 0:TT * D].rearrange("p (t d) -> p t d", t=TT)
                        if kind == "down" and layer == 1:
                            tt_op(X[s][:, :, :], y, X[s][:, :, :], ALU.add).then_inc(out_ready, 1)
                        else:
                            tt_op(X[s][:, :, :], y, X[s][:, :, :], ALU.add).then_inc(x_ready, 1)
                    elif kind == "up" and layer == 0:
                        dve.wait_ge(gelu, nth(gelu, task))
                        k = FF_B1 + i
                        nc.vector.scalar_tensor_tensor(hidden[:, i, :], b[:, 0:S], cols[:, k:k + 1], gate[:, counts.bank[task], :],
                                                       ALU.add, ALU.mult).then_inc(act0_ready, 1)


counts_side = ("prep", "vbias", "ctx", "ln", "g", "qk", "v", "mt", "r", "o", "up", "down")


def arrange(i):
    f = lambda name: np.asarray(i[name])
    heads_rows = lambda w, n: np.ascontiguousarray(w.T.reshape(HEADS, 64, n).transpose(1, 0, 2))
    a = {"x": f("x"), "ctx_768": f("ctx_768")}
    for k, n in (("sa", D), ("ca", DC)):
        a[f"wqT_{k}"] = heads_rows(f(f"L0_xattn_{k}_wq"), D)
        a[f"wkT_{k}"] = heads_rows(f(f"L0_xattn_{k}_wk"), n)
    a["wv0_sa"], a["wv0_ca"] = f("L0_xattn_sa_wv"), f("L0_xattn_ca_wv")
    a["wo0"] = np.stack([f(f"L0_xattn_{k}_wo").reshape(8, P, D) for k in ("sa", "ca")]).transpose(2, 0, 1, 3)
    a["w1_0"] = f("L0_xattn_ff_w1")
    a["w2_0"] = f("L0_xattn_ff_w2").reshape(4, P, D).transpose(1, 0, 2)
    order = [4 * r + c for c in range(4) for r in range(4)]
    in_slots = (np.arange(4) < 3)[None, :, None, None]
    slots = lambda w: np.where(in_slots, w.reshape(HEADS, 1, 8, -1)[order], np.zeros(1, w.dtype)).reshape(512, -1)
    pad = lambda w: np.concatenate([w.reshape(HEADS, 8, -1), np.zeros((HEADS, SLOT - 8, w.shape[-1] if w.ndim > 1 else 1), w.dtype)], 1).reshape(512, -1)
    q, k = [f(f"L1_xattn_sa_w{c}") for c in "qk"]
    a["wqk1_sa"] = np.stack([slots(q).T, slots(k).T], 1)
    a["wq1_ca"], a["wk1_ca"] = slots(f("L1_xattn_ca_wq")).T, slots(f("L1_xattn_ca_wk")).T
    a["wv1_sa"], a["wv1_ca"] = pad(f("L1_xattn_sa_wv")).T, pad(f("L1_xattn_ca_wv")).T
    a["wo1"] = np.stack([pad(f(f"L1_xattn_{c}_wo").T).reshape(4, P, D) for c in ("sa", "ca")]).transpose(2, 0, 1, 3)
    a["w1_1"] = f("L1_xattn_mlp_w1").T
    a["w2_1"] = f("L1_xattn_mlp_w2").T.reshape(4, P, D).transpose(1, 0, 2)
    cols = np.zeros((P, N_COLS), np.float32)
    for layer in range(2):
        for n in range(3):
            cols[:, LN_G + layer * 3 + n] = f(f"L{layer}_xattn_ln{n + 1}_g")
            cols[:, LN_B + layer * 3 + n] = f(f"L{layer}_xattn_ln{n + 1}_b")
    cols[:, FF_B1:FF_B1 + 8] = f("L0_xattn_ff_b1").reshape(8, P).T
    cols[:, MLP_B1:MLP_B1 + 4] = f("L1_xattn_mlp_b1").reshape(4, P).T
    low = {"q": np.array([0, 0, 1, 0]), "k": np.array([0, 1, 0, 0])}
    minus_m = np.isin(np.arange(P) % SLOT, (M_ROW, M_ROW + 1))
    for ci, c in enumerate(("sa", "ca")):
        for wi, w in enumerate("qk"):
            b = slots(f(f"L1_xattn_{c}_b{w}")).reshape(4, P).T
            is_low = np.repeat(np.tile(low[w], 4), 8) == 1
            n = (ci * 2 + wi) * 4
            cols[:, QK_B + n:QK_B + n + 4] = b
            cols[is_low, QK_BM + n:QK_BM + n + 4] = b[is_low]
            cols[is_low, MASK + wi] = 1
            if w == "k":
                cols[minus_m, QK_B + n:QK_B + n + 4] = -1
    a["cols"] = cols
    row_names = [f"L0_xattn_{n}" for n in ("sa_bo", "ca_bo", "ff_b2")] + [f"L1_xattn_{n}" for n in ("sa_bo", "ca_bo", "mlp_b2")]
    a["rows"] = np.broadcast_to(np.stack([f(n) for n in row_names]), (P, 6, D))
    vb = np.stack([pad(f(f"L1_xattn_{c}_bv"))[:, 0].reshape(4, P) for c in ("sa", "ca")])
    a["vcols"] = np.broadcast_to(vb.transpose(2, 0, 1)[:, :, :, None], (P, 2, 4, P))
    a["ident"] = np.eye(P, dtype=np.float32)
    selneg = np.zeros((P, PAIRS, P), np.float32)
    for t in range(PAIRS):
        selneg[[t, PAIRS + t], t] = -1
    e = np.zeros((P, QUADS, SLOT), np.float32)
    for q in range(QUADS):
        e[:, q, q] = 1
    e[:, 0, QUADS:] = 1
    sel0, sel1 = np.zeros((P, PAIRS, P), np.float32), np.zeros((P, QUADS, P), np.float32)
    for t in range(PAIRS):
        for par in range(2):
            sel0[SLOT * (2 * (t % 2) + par) + t // 2, t, 64 * par:64 * par + 64] = 1
    for c in range(QUADS):
        for j in range(4):
            sel1[SLOT * j + c, c, SLOT * j:SLOT * (j + 1)] = 1
    a["selneg"], a["e"], a["sel0"], a["sel1"] = selneg, e, sel0, sel1
    return a


def kernel(**inputs):
    import concourse.bacc as bacc
    from concourse.bass_utils import run_bass_kernel_spmd

    arrays = {f"in_{k}": np.ascontiguousarray(v) for k, v in arrange(inputs).items()}
    nc = bacc.Bacc("TRN2", target_bir_lowering=False, num_devices=1)
    args = [nc.dram_tensor(k, v.shape, mybir.dt.from_np(v.dtype), kind="ExternalInput").ap() for k, v in arrays.items()]
    out = nc.dram_tensor("out", (BATCHES, S, D), F32, kind="ExternalOutput").ap()
    build(nc, *args, out)
    r = run_bass_kernel_spmd(nc, [arrays], core_ids=[0])
    return r.results[0]["out"]
```
